# Optimizing a Trainium2 kernel written in Bass

```python
import numpy as np
import jax
import jax.numpy as jnp

def _softmax(x, axis=-1):
    return jax.nn.softmax(x, axis=axis)

def _gelu(x):
    return jax.nn.gelu(x, approximate=True)

def _silu(x):
    return jax.nn.silu(x)

def _sigmoid(x):
    return jax.nn.sigmoid(x)

def _layernorm(x, axis=-1, eps=1e-05):
    m = jnp.mean(x, axis=axis, keepdims=True)
    v = jnp.var(x, axis=axis, keepdims=True)
    return (x - m) / jnp.sqrt(v + eps)

def _scatter_add(tgt, idx, src, axis=0):
    return tgt.at[idx].add(src)

def _segment_sum(src, seg, n):
    return jax.ops.segment_sum(src, seg, n)
kernel_name = 'mk_gnn_resnorm_d2_gnn_r64_fb11b2'

def setup_inputs(seed: int=0):
    np.random.seed(seed)
    _w = jnp.asarray

    def _rec_inputs():
        import jax
        import jax.numpy as jnp
        _gk = jax.random.key(seed)
        x = -8.776e-05 + 1 * jax.random.normal(jax.random.fold_in(_gk, 1), (10000, 512), jnp.float32)
        src = jax.random.randint(jax.random.fold_in(_gk, 2), (2500,), 0, 10000, jnp.int32)
        dst = jnp.minimum((10000 * jax.random.uniform(jax.random.fold_in(_gk, 3), (2500,)) ** 2.0).astype(jnp.int32), 9999)
        _o = jnp.argsort(dst, stable=True)
        src = src[_o]
        dst = dst[_o]
        edge_weight = jax.random.uniform(jax.random.fold_in(_gk, 12), (2500,), jnp.float32, 0.0, 0.999996)
        return (x, src, dst, edge_weight)
    x, src, dst, edge_weight = _rec_inputs()

    def _L0_gnn_setup():
        import jax, jax.numpy as jnp
        import numpy as np
        N = 10000
        E = 2500
        D_IN = 512
        D_OUT = 512
        key = jax.random.key(seed)
        k1, k2, k3, k4, k5 = jax.random.split(key, 5)
        x = jax.random.normal(k1, (N, D_IN), dtype=jnp.float32)
        edge_index = jax.random.randint(k2, (2, E), 0, N, dtype=jnp.int64)
        edge_attr = jax.random.uniform(k3, (E,), dtype=jnp.float32)
        W = jax.random.normal(k4, (D_IN, D_OUT), dtype=jnp.float32) * 0.05
        b = jax.random.normal(k5, (D_OUT,), dtype=jnp.float32) * 0.05
        return {'x': x, 'edge_index': edge_index, 'edge_attr': edge_attr, 'W': W, 'b': b}
    _L0_gnn_all = _L0_gnn_setup()
    _L0_gnn_in = {k: v for k, v in _L0_gnn_all.items() if k in ('W', 'b')}
    del _L0_gnn_all

    def _L1_gnn_setup():
        import jax, jax.numpy as jnp
        import numpy as np
        N = 50000
        E = 6250
        D_IN = 512
        D_HID = 32
        D_OUT = 512
        key = jax.random.key(seed)
        k1, k2, k3, k4 = jax.random.split(key, 4)
        x = jax.random.normal(k1, (N, D_IN), dtype=jnp.float32)
        edge_index = jax.random.randint(k2, (2, E), 0, N, dtype=jnp.int64)
        W1 = jax.random.normal(k3, (D_IN, D_HID), dtype=jnp.float32) * (1.0 / np.sqrt(D_IN))
        b1 = jnp.zeros((D_HID,), dtype=jnp.float32)
        W2 = jax.random.normal(k4, (D_HID, D_OUT), dtype=jnp.float32) * (1.0 / np.sqrt(D_HID))
        b2 = jnp.zeros((D_OUT,), dtype=jnp.float32)
        return {'x': x, 'edge_index': edge_index, 'W1': W1, 'b1': b1, 'W2': W2, 'b2': b2}
    _L1_gnn_all = _L1_gnn_setup()
    _L1_gnn_in = {k: v for k, v in _L1_gnn_all.items() if k in ('W1', 'b1', 'W2', 'b2')}
    del _L1_gnn_all
    return {'x': x, 'src': src, 'dst': dst, 'edge_weight': edge_weight, 'L0_gnn_W': _L0_gnn_in['W'], 'L0_gnn_b': _L0_gnn_in['b'], 'L1_gnn_W1': _L1_gnn_in['W1'], 'L1_gnn_b1': _L1_gnn_in['b1'], 'L1_gnn_W2': _L1_gnn_in['W2'], 'L1_gnn_b2': _L1_gnn_in['b2']}

def reference(x, src, dst, edge_weight, L0_gnn_W, L0_gnn_b, L1_gnn_W1, L1_gnn_b1, L1_gnn_W2, L1_gnn_b2):
    import jax
    import jax.numpy as jnp

    def _L0_gnn_ref(x, edge_index, edge_attr, W, b):
        import jax, jax.numpy as jnp
        import numpy as np
        N = 10000
        E = 2500
        D_IN = 512
        D_OUT = 512
        n = x.shape[0]
        row, col = (edge_index[0], edge_index[1])
        loop = jnp.arange(n, dtype=edge_index.dtype)
        row_f = jnp.concatenate([row, loop])
        col_f = jnp.concatenate([col, loop])
        ew = jnp.concatenate([edge_attr, jnp.ones((n,), dtype=edge_attr.dtype)])
        deg = jax.ops.segment_sum(ew, col_f, num_segments=n)
        dinv = jnp.where(deg > 0, jax.lax.rsqrt(deg), 0.0)
        norm = dinv[row_f] * ew * dinv[col_f]
        h = x @ W
        msg = h[row_f] * norm[:, None]
        out = jax.ops.segment_sum(msg, col_f, num_segments=n)
        return out + b

    def _L1_gnn_ref(x, edge_index, W1, b1, W2, b2):
        import jax, jax.numpy as jnp
        import numpy as np
        N = 50000
        E = 6250
        D_IN = 512
        D_HID = 32
        D_OUT = 512
        h = jax.nn.relu(x @ W1 + b1) @ W2 + b2
        row, col = (edge_index[0], edge_index[1])
        agg = jax.ops.segment_sum(h[col], row, num_segments=h.shape[0])
        return h + agg
    edge_index = jnp.stack([src, dst])
    x = _layernorm(x + _L0_gnn_ref(x, edge_index, edge_weight, L0_gnn_W, L0_gnn_b), axis=-1)
    x = _layernorm(x + _L1_gnn_ref(x, edge_index, L1_gnn_W1, L1_gnn_b1, L1_gnn_W2, L1_gnn_b2), axis=-1)
    return x

_drawn_inputs = setup_inputs


def setup_inputs(seed=0):
    import zlib

    import numpy as np

    out = dict(_drawn_inputs(seed))
    spreads = {'L1_gnn_b1': (0.0, 0.1), 'L1_gnn_b2': (0.0, 0.1)}
    factors = {}
    for name, (base, spread) in spreads.items():
        noise = np.random.default_rng([zlib.crc32(name.encode()), seed]).standard_normal(out[name].shape)
        drawn = base * np.exp(spread * noise) if base else spread * noise
        out[name] = jnp.asarray(drawn.astype(out[name].dtype))
    for name, factor in factors.items():
        out[name] = (out[name] * factor).astype(out[name].dtype)
    return out
```

```python
from contextlib import ExitStack

import concourse.bass as bass
from concourse import mybir

F32 = mybir.dt.float32
F32R = mybir.dt.float32r
BF16 = mybir.dt.bfloat16
I32 = mybir.dt.int32
I16 = mybir.dt.int16
ALU = mybir.AluOpType
ACT = mybir.ActivationFunctionType

P = 128
EPS = 1e-5
SMALLEST_DEGREE = 1e-30
NO_ROW = 8192.0


def before(q, k, n, m):
    return q + (k - n) // m, (k - n) % m


def wait(eng, sem, value):
    if not isinstance(value, int) or value > 0:
        eng.wait_ge(sem, value)


def steps(eng, total, head, tail, m, step):
    assert head % m == 0
    rounds = (total - head - tail) // m
    for s in range(head):
        step(s // m, s % m)
    with eng.Fori(0, rounds) as r:
        for k in range(m):
            step(r + head // m, k)
    for s in range(head + rounds * m, total):
        step(s // m, s % m)


def graph_layers(nc, x, src, dst, ew, w, b, w1, b1, w2, b2, out):
    N, D = x.shape
    E = src.shape[0]
    H = w1.shape[1]
    KC = D // P
    NT = -(-N // P)
    TAIL = N - (NT - 1) * P
    ET = -(-E // P)
    EP = E // ET
    assert EP * ET == E and EP <= P and D == KC * P
    K2 = H + 1
    S3 = 3 * K2

    sums0 = nc.dram_tensor("edge_sums_0", (ET * P, D), F32).ap()
    sums1 = nc.dram_tensor("edge_sums_1", (ET * P, H), F32).ap()
    hidden = nc.dram_tensor("hidden", (N, H), F32).ap()

    with ExitStack() as ctx:
        def sb(name, shape, dt=F32):
            return ctx.enter_context(nc.sbuf_tensor(name, shape, dt))

        def sem(name):
            return ctx.enter_context(nc.semaphore(name))

        def sems(name, n):
            return [sem(f"{name}{i}") for i in range(n)]

        Y = sb("Y", [P, NT * D])
        taken = [12 * D]

        def scratch(words):
            at = taken[0]
            taken[0] += words
            assert taken[0] <= NT * D
            return Y[:, at:at + words]

        iota_col = scratch(P)
        iota_part = sb("iota_part", [P, 1])
        ident = sb("ident", [P, P])
        below = scratch(P)
        last_row = sb("last_row", [P, 1])
        ones = scratch(P)
        one = sb("one", [1, 1])
        eps = sb("eps", [P, 1])
        bias = sb("bias", [P, D])
        w_hi = sb("w_hi", [P, KC, D], F32R)
        w_lo = sb("w_lo", [P, KC, D], F32R)
        w1_sb = sb("w1_sb", [P, KC, H])
        b1_sb = sb("b1_sb", [1, H])
        dinv = sb("dinv", [P, NT])
        run_end = sb("run_end", [P, 2, NT], I32)
        fan = sb("fan", [P, NT])
        edge = sb("edge", [P, 2, 3, ET])
        edge_row = sb("edge_row", [P, 2, ET], I32)
        coef = scratch(ET)
        x_t = sb("x_t", [P, 2, D])
        z_t = sb("z_t", [P, 2, D])
        zT_hi = sb("zT_hi", [P, 2, KC, P], F32R)
        zT_lo = sb("zT_lo", [P, 2, KC, P], F32R)
        xb_t = sb("xb_t", [P, 2, D])
        y_t = sb("y_t", [P, 2, D])
        yT = sb("yT", [P, 2, KC, P])
        r_t = sb("r_t", [P, 2, H])
        end_idx = sb("end_idx", [P, 4], I32)
        stats = sb("stats", [P, 4, 6])
        mv = sb("mv", [P, 4, 2])
        sd = sb("sd", [P, 4])
        rstd = sb("rstd", [P, 4])
        shift = sb("shift", [P, 4])

        psum = ctx.enter_context(nc.psum_tensor("psum", [P, 8, 512], F32))

        key_col_i = scratch(2 * ET).bitcast(I32)[0:EP, :].rearrange("p (g t) -> p g t", g=2)
        ew_col = scratch(ET)[0:EP, :]
        cols = scratch(2 * ET)[0:EP, :].rearrange("p (g t) -> p g t", g=2)
        key_row_i = scratch(2 * E).bitcast(I32).rearrange("p (g e) -> p g e", g=2)
        twice = scratch(ET)[0:EP, :]
        row_keys = scratch(E // 2).bitcast(I16)
        greater = scratch(E).bitcast(BF16).rearrange("p (s e) -> p s e", s=2)
        tied = scratch(P).bitcast(BF16).rearrange("p (s e) -> p s e", s=2)
        ones16 = scratch(1).bitcast(BF16)
        zeros16 = scratch(P // 2).bitcast(BF16)
        ints = scratch(2 * ET).bitcast(I32).rearrange("p (s t) -> p s t", s=2)
        parts = scratch(2 * ET).rearrange("p (s t) -> p s t", s=2)
        hot_lo = scratch(ET * P).rearrange("p (t c) -> p t c", t=ET)
        hot_hi = scratch(ET * ET).rearrange("p (t c) -> p t c", t=ET)
        placed = scratch(3 * ET * ET).rearrange("p (t v c) -> p t v c", t=ET, v=3)
        node_hi = scratch(2 * ET * NT).rearrange("p (t v c) -> p t v c", t=ET, v=2)
        count_ = scratch(3 * NT).rearrange("p (s c) -> p s c", s=3)
        flat = scratch(2 * NT).rearrange("p (s c) -> p s c", s=2)
        lookup = scratch(2 * P).rearrange("p (s c) -> p s c", s=2)
        found = scratch(NT)
        src_inv = scratch(ET)
        gathered = scratch(ET * D).rearrange("p (t c) -> p t c", t=ET)
        w_f = scratch(KC * D).rearrange("p (c n) -> p c n", c=KC)
        same = xb_t[:, :, 0:P]
        open_run = xb_t[:, :, P:2 * P]
        sum_t = y_t
        prev_key = sb("prev_key", [P, 2])
        M2 = 4
        v_t = [x_t[:, 0, :], x_t[:, 1, :], xb_t[:, 0, :], xb_t[:, 1, :]]
        small = z_t[:, 0, :].rearrange("p (s c) -> p s c", s=M2)
        hid_t = small[:, :, 0:H]
        agg_t = small[:, :, H:2 * H]
        sum33 = z_t[:, 1, 0:M2 * K2].rearrange("p (s c) -> p s c", s=M2)
        w2_parts = w_hi[0:S3, 0, :]
        w2_f = x_t[0:S3, 0, :]
        w2_h = w_lo[0:S3, 1, :]
        w2_l = x_t[0:S3, 1, :]
        is_mid = y_t[0:S3, 0, D - 2:D]
        split = yT[:, 0, :, 0:S3]
        splitT = zT_hi[0:S3, 1, :, :]
        spare = (yT[:, 1, :, :].rearrange("p c n -> p (c n)"), z_t[:, 1, D // 2:D])

        def gathered1(t):
            per = D // H
            return spare[t // per][:, t % per * H:(t % per + 1) * H]

        edges_in = sem("edges_in")
        rows_in = sem("rows_in")
        weights_in = sem("weights_in")
        small_in = sem("small_in")
        w2_in = sem("w2_in")
        iotas_done = sem("iotas_done")
        dve_seq = sem("dve_seq")
        dve_consts = sem("dve_consts")
        row_key_down = sem("row_key_down")
        compared = sem("compared")
        counted = sem("counted")
        ranks_taken = sem("ranks_taken")
        placed_ready = sem("placed_ready")
        permuted = sem("permuted")
        hist_ready = sem("hist_ready")
        hist_done = sem("hist_done")
        prefix_ready = sem("prefix_ready")
        prefix_done = sem("prefix_done")
        degree_ready = sem("degree_ready")
        degree_root = sem("degree_root")
        dinv_ready = sem("dinv_ready")
        lo_row = sem("lo_row")
        lo_hot = sem("lo_hot")
        looked_up = sem("looked_up")
        look_taken = sem("look_taken")
        edges_sorted = sem("edges_sorted")
        coef_ready = sem("coef_ready")
        edge_rows_in = [sems("edge_rows_in", ET), sems("edge_hid_in", ET)]
        key_row = sem("key_row")
        same_ready = sem("same_ready")
        tile_summed = sem("tile_summed")
        sum_copied = sem("sum_copied")
        sum_stored = sems("sum_stored", 2)
        x_in = sems("x_in", 2)
        end_prep = sem("end_prep")
        acc_in = sems("acc_in", 2)
        xb_done = sem("xb_done")
        z_done = sem("z_done")
        zT_done = sem("zT_done")
        hi_done = sem("hi_done")
        lo_done = sem("lo_done")
        prod_done = sem("prod_done")
        u_done = sem("u_done")
        stats_done = sem("stats_done")
        mv_done = sem("mv_done")
        sd_done = sem("sd_done")
        rstd_done = sem("rstd_done")
        shift_done = sem("shift_done")
        y_done = sem("y_done")
        y_kept = sems("y_kept", 2)
        yT_done = sem("yT_done")
        yT_copied = sem("yT_copied")
        pre_done = sem("pre_done")
        r_done = sem("r_done")
        r_stored = sems("r_stored", 2)
        hid_in = sems("hid_in", M2)
        end_prep2 = sem("end_prep2")
        agg_in = sems("agg_in", M2)
        add_done = sem("add_done")
        hi2_done = sem("hi2_done")
        split_done = sem("split_done")
        splitT_done = sem("splitT_done")
        splitT_copied = sem("splitT_copied")
        prod2_done = sem("prod2_done")
        v_done = sem("v_done")
        stats2_done = sem("stats2_done")
        mv2_done = sem("mv2_done")
        sd2_done = sem("sd2_done")
        rstd2_done = sem("rstd2_done")
        shift2_done = sem("shift2_done")
        out_done = sem("out_done")
        out_stored = sems("out_stored", M2)

        block = ctx.enter_context(nc.Block())

        def times(sem_list, k, t_before, m):
            return sem_list[k], 16 * (t_before + 1)

        @block.sync
        def _(sp):
            for g, a in enumerate((dst, src)):
                sp.dma_start(key_col_i[:, g, :], a.rearrange("(p t) -> p t", p=EP)).then_inc(edges_in, 16)
            sp.dma_start(ew_col, ew.rearrange("(p t) -> p t", p=EP)).then_inc(edges_in, 16)
            for g, a in enumerate((dst, src)):
                sp.dma_start(key_row_i[:, g, :], a.rearrange("(a e) -> a e", a=1).to_broadcast([P, E])).then_inc(rows_in, 16)
            sp.dma_start(w_f, w.rearrange("(c p) n -> p c n", p=P)).then_inc(weights_in, 16)
            sp.dma_start(bias[:], b.rearrange("(a n) -> a n", a=1).to_broadcast([P, D])).then_inc(small_in, 16)
            sp.dma_start(w1_sb[:], w1.rearrange("(c p) n -> p c n", p=P)).then_inc(small_in, 16)
            sp.dma_start(b1_sb[:], b1.rearrange("(a n) -> a n", a=1)).then_inc(small_in, 16)

            def load_x(q, k):
                t = 2 * q + k
                wait(sp, z_done, t - 1)
                wait(sp, xb_done, t - 1)
                if isinstance(t, int) and t == NT - 1:
                    sp.dma_start(x_t[0:TAIL, k, :], x[t * P:N, :]).then_inc(x_in[k], 16)
                else:
                    sp.dma_start(x_t[:, k, :], x[bass.ds(t * P, P), :]).then_inc(x_in[k], 16)

            load_x(0, 0)
            load_x(0, 1)

            def store_sum(g, t):
                sp.wait_ge(sum_copied, g * ET + t + 1)
                dest, cols_ = ((sums0, D), (sums1, H))[g]
                sp.dma_start(dest[t * P:(t + 1) * P, :], sum_t[:, t % 2, 0:cols_]).then_inc(sum_stored[t % 2], 16)

            for t in range(ET):
                store_sum(0, t)

            def layer1_step(q, k):
                s = 2 * q + k
                static = isinstance(s, int)
                if not static or s + 2 < NT:
                    load_x(*before(q, k, -2, 2))
                if not static or 0 <= s - 2 < NT:
                    t, kk = s - 2, k
                    sp.wait_ge(y_done, t + 1)
                    sp.dma_start(Y[:, bass.ds(t * D, D)], y_t[:, kk, :]).then_inc(y_kept[kk], 16)
                if not static or 0 <= s - 4 < NT:
                    t, kk = s - 4, k
                    sp.wait_ge(r_done, t + 1)
                    if static and t == NT - 1:
                        sp.dma_start(hidden[t * P:N, :], r_t[0:TAIL, kk, :]).then_inc(r_stored[kk], 16)
                    else:
                        sp.dma_start(hidden[bass.ds(t * P, P), :], r_t[:, kk, :]).then_inc(r_stored[kk], 16)

            steps(sp, NT + 4, 6, 8, 2, layer1_step)

            sp.wait_ge(prod_done, NT)
            for c in range(3):
                sp.dma_start(w2_f[c * K2:c * K2 + H, :], w2).then_inc(w2_in, 16)
                sp.dma_start(w2_f[c * K2 + H:(c + 1) * K2, :], b2.rearrange("(a n) -> a n", a=1)).then_inc(w2_in, 16)

            for t in range(ET):
                store_sum(1, t)

            def load_hidden(q, k):
                t = M2 * q + k
                wait(sp, add_done, t - M2 + 1)
                if isinstance(t, int) and t == 0:
                    for kk in range(2):
                        sp.wait_ge(r_stored[kk], 16 * ((NT - kk + 1) // 2))
                if isinstance(t, int) and t == NT - 1:
                    sp.dma_start(hid_t[0:TAIL, k, :], hidden[t * P:N, :]).then_inc(hid_in[k], 16)
                else:
                    sp.dma_start(hid_t[:, k, :], hidden[bass.ds(t * P, P), :]).then_inc(hid_in[k], 16)

            for t in range(M2):
                load_hidden(0, t)

            def layer2_step(q, k):
                s = M2 * q + k
                static = isinstance(s, int)
                if not static or s + M2 < NT:
                    load_hidden(q + 1, k)
                if not static or 0 <= s - 1 < NT:
                    qq, kk = before(q, k, 1, M2)
                    t = s - 1
                    sp.wait_ge(out_done, t + 1)
                    if static and t == NT - 1:
                        sp.dma_start(out[t * P:N, :], v_t[kk][0:TAIL, :]).then_inc(out_stored[kk], 16)
                    else:
                        sp.dma_start(out[bass.ds(t * P, P), :], v_t[kk]).then_inc(out_stored[kk], 16)

            steps(sp, NT + 1, 2 * M2, M2 + 2, M2, layer2_step)
            for k in range(M2):
                sp.wait_ge(out_stored[k], 16 * ((NT - k + M2 - 1) // M2))

        @block.gpsimd
        def _(pool):
            pool.iota(iota_col, [[1, P]], base=0, channel_multiplier=0,
                      allow_small_or_imprecise_dtypes=True).then_inc(iotas_done, 1)
            pool.iota(iota_part[:], [[0, 1]], base=0, channel_multiplier=1,
                      allow_small_or_imprecise_dtypes=True).then_inc(iotas_done, 1)

            pool.wait_ge(edges_sorted, 1)
            for t in range(ET):
                pool.indirect_dma_start(gathered[:, t, :], None, x,
                                        bass.IndirectOffsetOnAxis(ap=edge_row[:, 0, t:t + 1], axis=0),
                                        bounds_check=N - 1, oob_is_err=False).then_inc(edge_rows_in[0][t], 16)

            last_sum = pool.to_reg(ET * P - 1)

            def node_sums(q, k):
                t = 2 * q + k
                static = isinstance(t, int)
                if not static or t < NT:
                    wait(pool, zT_done, t - 1)
                    pool.tensor_copy(end_idx[:, k:k + 1], run_end[:, 0, bass.ds(t, 1)]).then_inc(end_prep, 1)
                    pool.memset(z_t[:, k, :], 0.0).then_inc(end_prep, 1)
                    pool.wait_ge(end_prep, 2 * t + 2)
                if not static or t >= 2:
                    pool.wait_ge(x_in[k], 16 * q)
                    wait(pool, u_done, t - 3)
                    pool.tensor_tensor(xb_t[:, k, :], x_t[:, k, :], bias[:], ALU.add).then_inc(xb_done, 1)
                if not static or t < NT:
                    pool.indirect_dma_start(z_t[:, k, :], None, sums0,
                                            bass.IndirectOffsetOnAxis(ap=end_idx[:, k:k + 1], axis=0),
                                            bounds_check=last_sum, oob_is_err=False).then_inc(acc_in[k], 16)

            for k in range(2):
                pool.wait_ge(sum_stored[k], 16 * (ET // 2))
            pool.wait_ge(prefix_done, 4)
            pool.wait_ge(small_in, 16 * 3)
            steps(pool, NT + 2, 4, 3, 2, node_sums)

            for k in range(2):
                pool.wait_ge(r_stored[k], 16 * ((NT - k + 1) // 2))
            for t in range(ET):
                pool.indirect_dma_start(gathered1(t), None, hidden,
                                        bass.IndirectOffsetOnAxis(ap=edge_row[:, 1, t:t + 1], axis=0),
                                        bounds_check=N - 1, oob_is_err=False).then_inc(edge_rows_in[1][t], 16)

            def node_sums2(q, k):
                t = M2 * q + k
                static = isinstance(t, int)
                if not static or t >= 1:
                    wait(pool, end_prep2, 2 * t)
                if not static or t < NT:
                    wait(pool, add_done, t - M2 + 1)
                    pool.tensor_copy(end_idx[:, k:k + 1], run_end[:, 1, bass.ds(t, 1)]).then_inc(end_prep2, 1)
                    pool.memset(agg_t[:, k, :], 0.0).then_inc(end_prep2, 1)
                if not static or t >= 1:
                    kk = (k - 1) % M2
                    pool.indirect_dma_start(agg_t[:, kk, :], None, sums1,
                                            bass.IndirectOffsetOnAxis(ap=end_idx[:, kk:kk + 1], axis=0),
                                            bounds_check=last_sum, oob_is_err=False).then_inc(agg_in[kk], 16)

            for k in range(2):
                pool.wait_ge(sum_stored[k], 16 * ET)
            steps(pool, NT + 1, M2, 2, M2, node_sums2)

        @block.scalar
        def _(act):
            act.wait_ge(degree_ready, 1)
            nc.scalar.activation(count_[:, 2, :], count_[:, 2, :], ACT.Sqrt).then_inc(degree_root, 1)

            def copy_sum(g, t):
                act.wait_ge(tile_summed, g * ET + t + 1)
                n = g * (ET // 2) + t // 2
                wait(act, sum_stored[t % 2], 16 * n)
                c = (D, H)[g]
                nc.scalar.copy(sum_t[:, t % 2, 0:c], psum[:, 4 + t % 2, 0:c]).then_inc(sum_copied, 1)

            for t in range(ET):
                copy_sum(0, t)

            def layer1_step(q, k):
                s = 2 * q + k
                static = isinstance(s, int)
                if not static or s < NT:
                    act.wait_ge(zT_done, s + 1)
                    wait(act, prod_done, s - 1)
                    nc.scalar.copy(zT_hi[:, k, :, :].rearrange("p c n -> p (c n)"), psum[:, k, :]).then_inc(hi_done, 1)
                if not static or 0 <= s - 3 < NT:
                    t, kk = s - 3, (k - 3) % 2
                    act.wait_ge(yT_done, t + 1)
                    wait(act, pre_done, t - 1)
                    nc.scalar.copy(yT[:, kk, :, :].rearrange("p c n -> p (c n)"), psum[:, 4 + kk, :]).then_inc(yT_copied, 1)
                if not static or 0 <= s - 4 < NT:
                    t, kk = s - 4, k
                    act.wait_ge(pre_done, t + 1)
                    wait(act, r_stored[kk], 16 * (q - 2))
                    nc.scalar.activation(r_t[:, kk, :], psum[:, 6 + kk, 0:H], ACT.Relu).then_inc(r_done, 1)
                if not static or 0 <= s - 2 < NT:
                    t, kk = s - 2, k
                    act.wait_ge(mv_done, t + 1)
                    nc.scalar.activation(sd[:, kk:kk + 1], mv[:, kk, 1:2], ACT.Sqrt, bias=eps[:, 0:1]).then_inc(sd_done, 1)
                    act.wait_ge(shift_done, t + 1)
                    nc.scalar.activation(y_t[:, kk, :], y_t[:, kk, :], ACT.Identity, bias=shift[:, kk:kk + 1],
                                         scale=rstd[:, kk:kk + 1]).then_inc(y_done, 1)

            steps(act, NT + 4, 6, 5, 2, layer1_step)

            for t in range(ET):
                copy_sum(1, t)

            def layer2_step(q, k):
                s = M2 * q + k
                static = isinstance(s, int)
                if not static or s < NT:
                    act.wait_ge(splitT_done, s + 1)
                    wait(act, prod2_done, s - M2 + 1)
                    nc.scalar.copy(splitT[:, k, :], psum[0:S3, 4 + k % 2, 0:P]).then_inc(splitT_copied, 1)
                if not static or 0 <= s - 1 < NT:
                    t, kk = s - 1, (k - 1) % M2
                    act.wait_ge(mv2_done, t + 1)
                    nc.scalar.activation(sd[:, kk:kk + 1], mv[:, kk, 1:2], ACT.Sqrt, bias=eps[:, 0:1]).then_inc(sd2_done, 1)
                if not static or 0 <= s - 2 < NT:
                    t, kk = s - 2, (k - 2) % M2
                    act.wait_ge(shift2_done, t + 1)
                    nc.scalar.activation(v_t[kk], v_t[kk], ACT.Identity, bias=shift[:, kk:kk + 1],
                                         scale=rstd[:, kk:kk + 1]).then_inc(out_done, 1)

            steps(act, NT + 2, 2 * M2, 3, M2, layer2_step)

        @block.vector
        def _(dve):
            seq = [0]

            def then(ins):
                seq[0] += 1
                ins.then_inc(dve_seq, 1)
                dve.wait_ge(dve_seq, seq[0])

            dve.memset(ones, 1.0)
            dve.memset(one[:], 1.0)
            dve.memset(eps[:], EPS)
            dve.memset(ones16, 1.0)
            dve.memset(zeros16, 0.0)
            dve.memset(fan[:], 1.0)
            dve.wait_ge(iotas_done, 2)
            dve.tensor_scalar(ident[:], iota_col, iota_part[:, 0:1], None, ALU.is_equal)
            dve.tensor_scalar(below, iota_col, iota_part[:, 0:1], None, ALU.is_gt)
            then(dve.tensor_scalar(last_row[:], iota_part[:], float(P - 1), None, ALU.is_equal))
            dve.engine_nop().then_inc(dve_consts, 1) if False else dve.memset(prev_key[:], 0.0).then_inc(dve_consts, 1)
            dve.wait_ge(edges_in, 48)
            then(dve.tensor_copy(cols, key_col_i))

            def sort_edges(g):
                dve.wait_ge(rows_in, 32)
                dve.tensor_scalar(twice, cols[:, g, :], 2.0, None, ALU.mult)
                then(dve.tensor_scalar(row_keys.rearrange("q (t p) -> q t p", t=ET),
                                       key_row_i[:, g, :].rearrange("q (p t) -> q t p", t=ET),
                                       2.0, 1.0, ALU.mult, ALU.add))

                def compare(q, k):
                    t = 2 * q + k
                    n = g * ET + t
                    here = row_keys[0:EP, bass.ds(t * EP, EP)]
                    wait(dve, compared, n)
                    dve.tensor_scalar(here, here, 1.0, None, ALU.subtract).then_inc(row_key_down, 1)
                    dve.wait_ge(row_key_down, n + 1)
                    wait(dve, counted, n - 1)
                    dve.tensor_scalar(greater[0:EP, k, :], row_keys[0:EP, :], twice[:, bass.ds(t, 1)], None, ALU.is_gt)
                    dve.scalar_tensor_tensor(tied[0:EP, k, 0:EP], here, twice[:, bass.ds(t, 1)], below[0:EP, 0:EP],
                                             ALU.is_equal, ALU.mult).then_inc(compared, 1)

                steps(dve, ET, 2, 0, 2, compare)
                dve.wait_ge(counted, (g + 1) * ET)
                then(dve.tensor_copy(ints[0:EP, 0, :], psum[0:EP, 0, 0:ET]))
                dve.tensor_scalar(ints[0:EP, 1, :], ints[0:EP, 0, :], P - 1, None, ALU.bitwise_and)
                then(dve.tensor_scalar(ints[0:EP, 0, :], ints[0:EP, 0, :], 7, None, ALU.logical_shift_right))
                then(dve.tensor_copy(parts[0:EP], ints[0:EP]))
                dve.tensor_tensor(hot_lo[0:EP], iota_col[0:EP, None, 0:P].to_broadcast([EP, ET, P]),
                                  parts[0:EP, 1, :, None].to_broadcast([EP, ET, P]), ALU.is_equal)
                then(dve.tensor_tensor(hot_hi[0:EP], iota_col[0:EP, None, 0:ET].to_broadcast([EP, ET, ET]),
                                       parts[0:EP, 0, :, None].to_broadcast([EP, ET, ET]), ALU.is_equal))
                dve.tensor_tensor(placed[0:EP, :, 0, :], hot_hi[0:EP],
                                  cols[:, g, :, None].to_broadcast([EP, ET, ET]), ALU.mult)
                last = dve.tensor_tensor(placed[0:EP, :, 1, :], hot_hi[0:EP],
                                         cols[:, 1 - g, :, None].to_broadcast([EP, ET, ET]), ALU.mult)
                if g == 0:
                    last = dve.tensor_tensor(placed[0:EP, :, 2, :], hot_hi[0:EP],
                                             ew_col[:, :, None].to_broadcast([EP, ET, ET]), ALU.mult)
                else:
                    last = dve.tensor_copy(placed[0:EP, :, 2, :], hot_hi[0:EP])
                last.then_inc(placed_ready, 1)
                dve.wait_ge(permuted, g + 1)
                then(dve.tensor_copy(edge[:, g, :, :].rearrange("p v t -> p (v t)"), psum[:, 1, 0:3 * ET]))
                dve.tensor_copy(edge_row[:, g, :], edge[:, g, 1, :]).then_inc(edges_sorted, 1)

            def count_nodes(g):
                then(dve.tensor_copy(ints[0:EP, 0, :], cols[:, g, :]))
                dve.tensor_scalar(ints[0:EP, 1, :], ints[0:EP, 0, :], P - 1, None, ALU.bitwise_and)
                then(dve.tensor_scalar(ints[0:EP, 0, :], ints[0:EP, 0, :], 7, None, ALU.logical_shift_right))
                then(dve.tensor_copy(parts[0:EP], ints[0:EP]))
                dve.tensor_tensor(hot_lo[0:EP], iota_col[0:EP, None, 0:P].to_broadcast([EP, ET, P]),
                                  parts[0:EP, 1, :, None].to_broadcast([EP, ET, P]), ALU.is_equal)
                then(dve.tensor_tensor(node_hi[0:EP, :, 0, :], iota_col[0:EP, None, 0:NT].to_broadcast([EP, ET, NT]),
                                       parts[0:EP, 0, :, None].to_broadcast([EP, ET, NT]), ALU.is_equal))
                dve.tensor_tensor(node_hi[0:EP, :, 1, :], node_hi[0:EP, :, 0, :],
                                  ew_col[:, :, None].to_broadcast([EP, ET, NT]), ALU.mult).then_inc(hist_ready, 1)
                dve.wait_ge(hist_done, g + 1)
                then(dve.tensor_copy(count_[:, 0:2, :].rearrange("p v c -> p (v c)"), psum[:, 2, 0:2 * NT]))
                if g == 0:
                    then(dve.tensor_scalar(count_[:, 1, :], count_[:, 1, :], 1.0, None, ALU.add))
                    dve.tensor_scalar(count_[:, 2, :], count_[:, 1, :], SMALLEST_DEGREE, None,
                                      ALU.max).then_inc(degree_ready, 1)
                else:
                    dve.tensor_scalar(fan[:], count_[:, 0, :], 1.0, None, ALU.add)
                then(dve.memset(flat[:, 0, 0:1], 0.0))
                then(dve.tensor_copy(flat[:, 0, 1:NT], count_[:, 0, 0:NT - 1]))
                at, width = 0, 1
                while width < NT:
                    dve.tensor_copy(flat[:, 1 - at, 0:width], flat[:, at, 0:width])
                    then(dve.tensor_tensor(flat[:, 1 - at, width:NT], flat[:, at, width:NT],
                                           flat[:, at, 0:NT - width], ALU.add))
                    at, width = 1 - at, 2 * width
                dve.memset(found, 0.0).then_inc(prefix_ready, 1)
                assert at == 1
                dve.tensor_scalar(flat[:, 0, :], count_[:, 0, :], 0.0, NO_ROW, ALU.is_equal, ALU.mult).then_inc(prefix_done, 1)
                dve.wait_ge(prefix_ready, 2 * g + 2)
                dve.wait_ge(prefix_done, 2 * g + 1)
                dve.scalar_tensor_tensor(run_end[:, g, :], psum[:, 3, 0:NT], -1.0, flat[:, 0, :],
                                         ALU.add, ALU.add).then_inc(prefix_done, 1)
                if g == 0:
                    dve.wait_ge(degree_root, 1)
                    then(dve.reciprocal(found, count_[:, 2, :]))
                    then(dve.scalar_tensor_tensor(dinv[:], count_[:, 1, :], 0.0, found, ALU.is_gt, ALU.mult))

            def edge_weights():
                then(dve.tensor_scalar(ints[:, 1, :], edge_row[:, 0, :], P - 1, None, ALU.bitwise_and))
                then(dve.tensor_scalar(ints[:, 0, :], edge_row[:, 0, :], 7, None, ALU.logical_shift_right))
                dve.tensor_copy(parts, ints).then_inc(dinv_ready, 1)
                dve.wait_ge(dinv_ready, 1)
                for t in range(ET):
                    k = t % 2
                    dve.wait_ge(lo_row, t + 1)
                    dve.tensor_scalar(lookup[:, k, :], psum[:, 4 + k, 0:P], iota_part[:, 0:1], None,
                                      ALU.is_equal).then_inc(lo_hot, 1)
                    dve.wait_ge(looked_up, t + 1)
                    dve.scalar_tensor_tensor(found, iota_col[:, 0:NT], parts[:, 0, t:t + 1], psum[:, 6 + k, 0:NT],
                                             ALU.is_equal, ALU.mult, accum_out=src_inv[:, t:t + 1]).then_inc(look_taken, 1)
                dve.wait_ge(look_taken, ET)
                then(dve.tensor_tensor(coef, edge[:, 0, 2, :], src_inv, ALU.mult))

            def match_keys(g):
                for t in range(ET):
                    k, n = t % 2, g * ET + t
                    weight = (coef[:, t:t + 1], edge[:, 1, 2, t:t + 1])[g]
                    dve.wait_ge(key_row, n + 1)
                    wait(dve, tile_summed, n - 1)
                    dve.tensor_scalar(same[:, k, :], psum[:, k, 0:P], edge[:, g, 0, t:t + 1], weight,
                                      ALU.is_equal, ALU.mult)
                    if t > 0:
                        dve.tensor_scalar(open_run[:, k, :], psum[:, k, 0:P], prev_key[:, 1 - k:2 - k], last_row[:, 0:1],
                                          ALU.is_equal, ALU.mult)
                    dve.tensor_copy(prev_key[:, k:k + 1], psum[:, k, P - 1:P]).then_inc(same_ready, 1)
                    dve.wait_ge(same_ready, n + 1)

            sort_edges(0)
            count_nodes(0)
            edge_weights()
            sort_edges(1)
            count_nodes(1)
            dve.wait_ge(weights_in, 16)
            then(dve.tensor_copy(w_hi[:], w_f))
            dve.tensor_tensor(w_lo[:], w_f, w_hi[:].bitcast(F32), ALU.subtract)
            match_keys(0)

            def make_z(q, k):
                dve.wait_ge(x_in[k], 16 * (q + 1))
                dve.wait_ge(acc_in[k], 16 * (q + 1))
                t = 2 * q + k
                dve.scalar_tensor_tensor(z_t[:, k, :], x_t[:, k, :], dinv[:, bass.ds(t, 1)], z_t[:, k, :],
                                         ALU.mult, ALU.add).then_inc(z_done, 1)

            make_z(0, 0)

            def layer1_step(q, k):
                s = 2 * q + k
                static = isinstance(s, int)
                has_u = not static or 0 <= s - 2 < NT
                t, kk = s - 2, k
                if has_u:
                    dve.wait_ge(prod_done, t + 1)
                    dve.wait_ge(xb_done, t + 1)
                    wait(dve, yT_done, t - 1)
                    wait(dve, y_kept[kk], 16 * (q - 1))
                    dve.scalar_tensor_tensor(y_t[:, kk, :], psum[:, 2 + kk, :], dinv[:, bass.ds(t, 1)], xb_t[:, kk, :],
                                             ALU.mult, ALU.add).then_inc(u_done, 1)
                    dve.wait_ge(u_done, t + 1)
                    dve.bn_stats(stats[:, kk, :], y_t[:, kk, :]).then_inc(stats_done, 1)
                    dve.wait_ge(iotas_done, 2)
                    dve.wait_ge(stats_done, t + 1)
                    dve.bn_aggr(mv[:, kk, :], stats[:, kk, :]).then_inc(mv_done, 1)
                if not static or s < NT:
                    dve.wait_ge(hi_done, s + 1)
                    wait(dve, prod_done, s - 1)
                    dve.tensor_tensor(zT_lo[:, k, :, :].rearrange("p c n -> p (c n)"), psum[:, k, :],
                                      zT_hi[:, k, :, :].rearrange("p c n -> p (c n)").bitcast(F32),
                                      ALU.subtract).then_inc(lo_done, 1)
                if has_u:
                    dve.wait_ge(sd_done, t + 1)
                    wait(dve, y_done, t - 1)
                    dve.reciprocal(rstd[:, kk:kk + 1], sd[:, kk:kk + 1]).then_inc(rstd_done, 1)
                    dve.wait_ge(rstd_done, t + 1)
                    dve.scalar_tensor_tensor(shift[:, kk:kk + 1], mv[:, kk, 0:1], -1.0, rstd[:, kk:kk + 1],
                                             ALU.mult, ALU.mult).then_inc(shift_done, 1)
                if not static or s + 1 < NT:
                    make_z(*before(q, k, -1, 2))

            steps(dve, NT + 4, 6, 5, 2, layer1_step)

            dve.wait_ge(prod_done, NT)
            match_keys(1)
            dve.wait_ge(w2_in, 16 * 6)
            then(dve.tensor_copy(w2_h, w2_f))
            dve.tensor_scalar(is_mid[:, 0:1], iota_part[0:S3, :], float(K2), None, ALU.is_ge)
            then(dve.tensor_scalar(is_mid[:, 1:2], iota_part[0:S3, :], float(2 * K2), None, ALU.is_lt))
            then(dve.tensor_tensor(is_mid[:, 0:1], is_mid[:, 0:1], is_mid[:, 1:2], ALU.mult))
            then(dve.tensor_scalar(is_mid[:, 1:2], is_mid[:, 0:1], -1.0, 1.0, ALU.mult, ALU.add))
            then(dve.tensor_tensor(w2_l, w2_f, w2_h.bitcast(F32), ALU.subtract))
            then(dve.tensor_scalar(w2_l, w2_l, is_mid[:, 0:1], None, ALU.mult))
            then(dve.scalar_tensor_tensor(w2_parts, w2_h.bitcast(F32), is_mid[:, 1:2], w2_l, ALU.mult, ALU.add))

            def make_split(q, k):
                t = M2 * q + k
                dve.wait_ge(hid_in[k], 16 * (q + 1))
                dve.wait_ge(agg_in[k], 16 * (q + 1))
                dve.tensor_copy(sum33[:, k, H:K2], fan[:, bass.ds(t, 1)])
                dve.tensor_tensor(sum33[:, k, 0:H], hid_t[:, k, :], agg_t[:, k, :], ALU.add).then_inc(add_done, 1)
                dve.wait_ge(add_done, t + 1)
                wait(dve, splitT_done, t - M2 + 1)
                halves = split[:, k, :].rearrange("p (s c) -> p s c", s=3)
                dve.tensor_copy(halves[:, 0:2, :].bitcast(F32R),
                                sum33[:, k, None, :].to_broadcast([P, 2, K2])).then_inc(hi2_done, 1)
                dve.wait_ge(hi2_done, t + 1)
                dve.tensor_tensor(halves[:, 2, :].bitcast(F32R), sum33[:, k, :], halves[:, 0, :], ALU.subtract).then_inc(split_done, 1)

            make_split(0, 0)
            make_split(0, 1)

            def layer2_step(q, k):
                s = M2 * q + k
                static = isinstance(s, int)
                if not static or s + 2 < NT:
                    make_split(*before(q, k, -2, M2))
                if not static or s < NT:
                    t = s
                    dve.wait_ge(prod2_done, t + 1)
                    wait(dve, out_stored[k], 16 * q)
                    dve.tensor_tensor(v_t[k], psum[:, k, :], Y[:, bass.ds(t * D, D)], ALU.add).then_inc(v_done, 1)
                    dve.wait_ge(v_done, t + 1)
                    dve.bn_stats(stats[:, k, :], v_t[k]).then_inc(stats2_done, 1)
                    dve.wait_ge(iotas_done, 2)
                    dve.wait_ge(stats2_done, t + 1)
                    dve.bn_aggr(mv[:, k, :], stats[:, k, :]).then_inc(mv2_done, 1)
                if not static or 0 <= s - 1 < NT:
                    t, kk = s - 1, (k - 1) % M2
                    dve.wait_ge(sd2_done, t + 1)
                    wait(dve, out_done, t - M2 + 1)
                    dve.reciprocal(rstd[:, kk:kk + 1], sd[:, kk:kk + 1]).then_inc(rstd2_done, 1)
                    dve.wait_ge(rstd2_done, t + 1)
                    dve.scalar_tensor_tensor(shift[:, kk:kk + 1], mv[:, kk, 0:1], -1.0, rstd[:, kk:kk + 1],
                                             ALU.mult, ALU.mult).then_inc(shift2_done, 1)

            steps(dve, NT + 1, 2 * M2, 4, M2, layer2_step)

        @block.tensor
        def _(pe):
            pe.wait_ge(dve_consts, 1)

            def count_ranks(g):
                pe.matmul(psum[0:EP, 0, 0:ET], zeros16[0:EP, 0:EP], zeros16[0:EP, 0:ET], start=True, stop=False,
                          skip_group_check=True)

                def count(q, k):
                    t = 2 * q + k
                    pe.wait_ge(compared, g * ET + t + 1)
                    for c in range(ET):
                        pe.matmul(psum[0:EP, 0, c:c + 1], greater[0:EP, k, c * EP:(c + 1) * EP], ones16[0:EP, 0:1],
                                  start=False, stop=False, skip_group_check=True)
                    pe.matmul(psum[0:EP, 0, bass.ds(t, 1)], tied[0:EP, k, 0:EP], ones16[0:EP, 0:1],
                              start=False, stop=False, skip_group_check=True).then_inc(counted, 1)

                steps(pe, ET, 2, 0, 2, count)
                pe.wait_ge(placed_ready, g + 1)
                for t in range(ET):
                    mm = pe.matmul(psum[:, 1, 0:3 * ET], hot_lo[0:EP, t, :],
                                   placed[0:EP, t, :, :].rearrange("p v c -> p (v c)"), start=t == 0, stop=t == ET - 1)
                mm.then_inc(permuted, 1)
                pe.wait_ge(hist_ready, g + 1)
                for t in range(ET):
                    mm = pe.matmul(psum[:, 2, 0:2 * NT], hot_lo[0:EP, t, :],
                                   node_hi[0:EP, t, :, :].rearrange("p v c -> p (v c)"), start=t == 0, stop=t == ET - 1)
                mm.then_inc(hist_done, 1)
                pe.wait_ge(prefix_ready, 2 * g + 1)
                pe.matmul(psum[:, 3, 0:NT], ones, flat[:, 1, :], start=True, stop=False)
                pe.matmul(psum[:, 3, 0:NT], below, count_[:, 0, :], start=False, stop=False)
                pe.matmul(psum[:, 3, 0:NT], ident[:], count_[:, 0, :], start=False, stop=True).then_inc(prefix_ready, 1)

            def row_of(out_ap, column):
                return pe.matmul(out_ap, column.to_broadcast([P, P]), ident[:], start=True, stop=True)

            def look_up():
                pe.wait_ge(dinv_ready, 1)
                row_of(psum[:, 4, 0:P], parts[:, 1, 0:1]).then_inc(lo_row, 1)
                for t in range(ET):
                    k = t % 2
                    if t + 1 < ET:
                        wait(pe, lo_hot, t)
                        row_of(psum[:, 5 - k, 0:P], parts[:, 1, t + 1:t + 2]).then_inc(lo_row, 1)
                    pe.wait_ge(lo_hot, t + 1)
                    wait(pe, look_taken, t - 1)
                    pe.matmul(psum[:, 6 + k, 0:NT], lookup[:, k, :], dinv[:], start=True, stop=True).then_inc(looked_up, 1)

            def sum_runs(g):
                c = (D, H)[g]
                if g == 0:
                    pe.wait_ge(edges_sorted, 1)
                    pe.wait_ge(look_taken, ET)
                row_of(psum[:, 0, 0:P], edge[:, g, 0, 0:1]).then_inc(key_row, 1)
                for t in range(ET):
                    k, n = t % 2, g * ET + t
                    if t + 1 < ET:
                        wait(pe, same_ready, n)
                        row_of(psum[:, 1 - k, 0:P], edge[:, g, 0, t + 1:t + 2]).then_inc(key_row, 1)
                    pe.wait_ge(same_ready, n + 1)
                    pe.wait_ge(edge_rows_in[g][t], 16)
                    wait(pe, sum_copied, n - 1)
                    rows = gathered[:, t, :] if g == 0 else gathered1(t)
                    mm = pe.matmul(psum[:, 4 + k, 0:c], same[:, k, :], rows, start=True, stop=t == 0)
                    if t > 0:
                        pe.wait_ge(sum_copied, n)
                        mm = pe.matmul(psum[:, 4 + k, 0:c], open_run[:, k, :], sum_t[:, 1 - k, 0:c], start=False, stop=True)
                    mm.then_inc(tile_summed, 1)

            count_ranks(0)
            look_up()
            pe.wait_ge(edges_sorted, 1)
            count_ranks(1)
            sum_runs(0)

            def layer1_step(q, k):
                s = 2 * q + k
                static = isinstance(s, int)
                if not static or s < NT:
                    pe.wait_ge(z_done, s + 1)
                    wait(pe, hi_done, s - 1)
                    wait(pe, lo_done, s - 1)
                    for c in range(KC):
                        mm = pe.transpose(psum[:, k, c * P:(c + 1) * P], z_t[:, k, c * P:(c + 1) * P], ident[:])
                    mm.then_inc(zT_done, 1)
                if not static or 0 <= s - 3 < NT:
                    t, kk = s - 3, (k - 3) % 2
                    pe.wait_ge(y_done, t + 1)
                    wait(pe, yT_copied, t - 1)
                    for c in range(KC):
                        mm = pe.transpose(psum[:, 4 + kk, c * P:(c + 1) * P], y_t[:, kk, c * P:(c + 1) * P], ident[:])
                    mm.then_inc(yT_done, 1)
                if not static or 0 <= s - 1 < NT:
                    t, kk = s - 1, (k - 1) % 2
                    pe.wait_ge(hi_done, t + 1)
                    pe.wait_ge(lo_done, t + 1)
                    wait(pe, u_done, t - 1)
                    n = 0
                    for c in range(KC):
                        for a, bb in ((zT_hi, w_hi), (zT_hi, w_lo), (zT_lo, w_hi)):
                            mm = pe.matmul(psum[:, 2 + kk, :], a[:, kk, c, :], bb[:, c, :], start=n == 0, stop=n == 3 * KC - 1)
                            n += 1
                    mm.then_inc(prod_done, 1)
                if not static or 0 <= s - 3 < NT:
                    t, kk = s - 3, (k - 3) % 2
                    pe.wait_ge(yT_copied, t + 1)
                    wait(pe, r_done, t - 1)
                    pre = psum[:, 6 + kk, 0:H]
                    pe.matmul(pre, one[:].to_broadcast([1, P]), b1_sb[:], start=True, stop=False)
                    for c in range(KC):
                        mm = pe.matmul(pre, yT[:, kk, c, :], w1_sb[:, c, :], start=False, stop=c == KC - 1)
                    mm.then_inc(pre_done, 1)

            pe.wait_ge(same_ready, 1)
            pe.wait_ge(small_in, 16 * 3)
            steps(pe, NT + 4, 6, 5, 2, layer1_step)

            sum_runs(1)

            def transpose_split(q, k):
                t = M2 * q + k
                pe.wait_ge(split_done, t + 1)
                wait(pe, splitT_copied, t - 1)
                pe.transpose(psum[0:S3, 4 + k % 2, 0:P], split[:, k, :], ident[:]).then_inc(splitT_done, 1)

            transpose_split(0, 0)

            def layer2_step(q, k):
                s = M2 * q + k
                static = isinstance(s, int)
                if not static or s + 1 < NT:
                    transpose_split(*before(q, k, -1, M2))
                pe.wait_ge(splitT_copied, s + 1)
                wait(pe, v_done, s - M2 + 1)
                pe.matmul(psum[:, k, :], splitT[:, k, :], w2_parts, start=True, stop=True).then_inc(prod2_done, 1)

            steps(pe, NT, 2 * M2, 3, M2, layer2_step)


_INS = ['x', 'src', 'dst', 'edge_weight', 'L0_gnn_W', 'L0_gnn_b', 'L1_gnn_W1', 'L1_gnn_b1', 'L1_gnn_W2', 'L1_gnn_b2']


def kernel(**inputs):
    import numpy as _np
    import concourse.bacc as _bacc
    from concourse import mybir as _mybir
    from concourse.bass_utils import run_bass_kernel_spmd as _run

    nc = _bacc.Bacc("TRN2", target_bir_lowering=False, num_devices=1)
    arrays, args = {}, []
    for name in _INS:
        a = _np.ascontiguousarray(inputs[name])
        arrays[f"in_{name}_dram"] = a
        args.append(nc.dram_tensor(f"in_{name}_dram", a.shape, _mybir.dt.from_np(a.dtype), kind="ExternalInput").ap())
    out = nc.dram_tensor("out_0_dram", inputs["x"].shape, _mybir.dt.float32, kind="ExternalOutput").ap()
    graph_layers(nc, *args, out)
    r = _run(nc, [arrays], core_ids=[0])
    return r.results[0]["out_0_dram"]
```

```python
from contextlib import ExitStack

import concourse.bass as bass
from concourse import mybir

F32 = mybir.dt.float32
F32R = mybir.dt.float32r
BF16 = mybir.dt.bfloat16
I32 = mybir.dt.int32
I16 = mybir.dt.int16
ALU = mybir.AluOpType
ACT = mybir.ActivationFunctionType
AXIS = mybir.AxisListType

P = 128
EPS = 1e-5
SMALLEST_DEGREE = 1e-30
NO_ROW = 8192.0


def before(q, k, n, m):
    return q + (k - n) // m, (k - n) % m


def wait(eng, sem, value):
    if not isinstance(value, int) or value > 0:
        eng.wait_ge(sem, value)


def steps(eng, total, head, tail, m, step):
    assert head % m == 0
    rounds = (total - head - tail) // m
    for s in range(head):
        step(s // m, s % m)
    with eng.Fori(0, rounds) as r:
        for k in range(m):
            step(r + head // m, k)
    for s in range(head + rounds * m, total):
        step(s // m, s % m)


def graph_layers(nc, x, src, dst, ew, w, b, w1, b1, w2, b2, out):
    N, D = x.shape
    E = src.shape[0]
    H = w1.shape[1]
    KC = D // P
    NT = -(-N // P)
    TAIL = N - (NT - 1) * P
    ET = -(-E // P)
    EP = E // ET
    assert EP * ET == E and EP <= P and D == KC * P
    PER = 4
    CHUNK = PER * EP
    CHUNKS = ET // PER
    assert CHUNKS * PER == ET and CHUNK <= 512 and CHUNKS <= 5
    LOOKS = 512 // NT
    K2 = H + 1
    S3 = 3 * K2

    sums0 = nc.dram_tensor("edge_sums_0", (ET * P, D), F32).ap()
    sums1 = nc.dram_tensor("edge_sums_1", (ET * P, H), F32).ap()
    hidden = nc.dram_tensor("hidden", (N, H), F32).ap()

    with ExitStack() as ctx:
        def sb(name, shape, dt=F32):
            return ctx.enter_context(nc.sbuf_tensor(name, shape, dt))

        def sem(name):
            return ctx.enter_context(nc.semaphore(name))

        def sems(name, n):
            return [sem(f"{name}{i}") for i in range(n)]

        Y = sb("Y", [P, NT * D])
        taken = [0]

        def scratch(words):
            at = taken[0]
            taken[0] += words
            assert taken[0] <= NT * D
            return Y[:, at:at + words]

        iota_col = scratch(P)
        iota_part = sb("iota_part", [P, 1])
        ident = sb("ident", [P, P])
        below = scratch(P)
        last_row = sb("last_row", [P, 1])
        ones = scratch(P)
        eps = sb("eps", [P, 1])
        bias = sb("bias", [P, D])
        w_hi = sb("w_hi", [P, KC, D], F32R)
        w_lo = sb("w_lo", [P, KC, D], F32R)
        w1_sb = sb("w1_sb", [P, KC, H])
        b1_sb = sb("b1_sb", [P, H])
        dinv = sb("dinv", [P, NT])
        run_end = sb("run_end", [P, 2, NT + 1], I32)
        fan = sb("fan", [P, NT + 1])
        edge = sb("edge", [P, 2, 3, ET])
        edge_row = sb("edge_row", [P, 2, ET], I32)
        x_t = sb("x_t", [P, 2, D])
        z_t = sb("z_t", [P, 2, D])
        zT_hi = sb("zT_hi", [P, 2, KC, P], F32R)
        zT_lo = sb("zT_lo", [P, 2, KC, P], F32R)
        xb_t = sb("xb_t", [P, 2, D])
        y_t = sb("y_t", [P, 2, D])
        yT = sb("yT", [P, 2, KC, P])
        r_t = sb("r_t", [P, 2, H])
        end_idx = sb("end_idx", [P, 8], I32)
        stats = sb("stats", [P, 8, 6])
        mv = sb("mv", [P, 8, 2])
        sd = sb("sd", [P, 8])
        rstd = sb("rstd", [P, 8])
        shift = sb("shift", [P, 8])

        psum = ctx.enter_context(nc.psum_tensor("psum", [P, 8, 512], F32))

        key_col_i = scratch(2 * ET).bitcast(I32)[0:EP, :].rearrange("p (g t) -> p g t", g=2)
        ew_col = scratch(ET)[0:EP, :]
        cols = scratch(2 * ET)[0:EP, :].rearrange("p (g t) -> p g t", g=2)
        key_row_i = scratch(2 * E).bitcast(I32).rearrange("p (g e) -> p g e", g=2)
        twice = scratch(ET)[0:EP, :]
        row_keys = scratch(E // 2).bitcast(I16)
        greater_words = scratch(E)
        greater = greater_words.bitcast(BF16).rearrange("p (s e) -> p s e", s=2)
        tied = scratch(P).bitcast(BF16).rearrange("p (s e) -> p s e", s=2)
        ones16 = scratch(P // 2).bitcast(BF16)
        iota16 = scratch(P // 2).bitcast(BF16)
        ints = scratch(4 * ET).bitcast(I32).rearrange("p (s g t) -> p s g t", s=2, g=2)
        parts = scratch(4 * ET).rearrange("p (s g t) -> p s g t", s=2, g=2)
        rank_ints = scratch(2 * ET).bitcast(I32).rearrange("p (s t) -> p s t", s=2)
        ranks = scratch(ET)
        diagonal = greater_words[0:EP, :].rearrange("p (t e) -> p t e", t=ET)
        rank_parts = scratch(ET).bitcast(BF16).rearrange("p (s t) -> p s t", s=2)
        parts16 = scratch(2 * ET).bitcast(BF16).rearrange("p (v t) -> p v t", v=4)
        hot_lo = scratch(ET * P // 2).bitcast(BF16).rearrange("p (t c) -> p t c", t=ET)
        hot_hi = scratch(ET * ET // 2).bitcast(BF16).rearrange("p (t c) -> p t c", t=ET)
        placed = scratch(5 * ET * ET // 2).bitcast(BF16).rearrange("p (t v c) -> p t v c", t=ET, v=5)
        placed_weights = scratch(3 * ET * ET // 2).bitcast(BF16).rearrange("p (t v c) -> p t v c", t=ET, v=3)
        sorted_parts = scratch(4 * ET).rearrange("p (h g t) -> p h g t", h=2, g=2)
        gathered_words = scratch(ET * D)
        gathered = gathered_words.rearrange("p (t c) -> p t c", t=ET)
        node_lo = [gathered_words[:, ET * (D - P):].rearrange("p (t c) -> p t c", t=ET),
                   scratch(ET * P // 2).bitcast(BF16).rearrange("p (t c) -> p t c", t=ET)]
        node_values = scratch(2 * ET * NT).rearrange("p (t v c) -> p t v c", t=ET, v=2)
        src_hi = scratch(ET * NT // 2).bitcast(BF16).rearrange("p (t c) -> p t c", t=ET)
        count_ = scratch(2 * NT).rearrange("p (g c) -> p g c", g=2)
        degree = scratch(2 * NT).rearrange("p (s c) -> p s c", s=2)
        half = scratch(NT)
        guess = scratch(NT)
        flat = scratch(4 * NT).rearrange("p (s g c) -> p s g c", s=2, g=2)
        row_lo = key_row_i[:, 0, :]
        src_hot = scratch(E // 2).bitcast(BF16)
        dinv_parts = scratch(3 * NT // 2 + 1).bitcast(BF16)[:, 0:3 * NT].rearrange("p (v c) -> p v c", v=3)
        rest = scratch(NT)
        look_prod = scratch(ET * NT).rearrange("p (t c) -> p t c", t=ET)
        weight_parts = scratch(3 * ET // 2).bitcast(BF16).rearrange("p (v t) -> p v t", v=3)
        src_inv = scratch(ET)
        w_f = scratch(KC * D).rearrange("p (c n) -> p c n", c=KC)
        ends2 = run_end[:, 1, :]
        same = xb_t[:, :, 0:P]
        open_run = xb_t[:, :, P:2 * P]
        sum_t = y_t
        prev_key = sb("prev_key", [P, 2])
        M2 = 4
        NG = -(-NT // M2)
        LAST = NT - (NG - 1) * M2
        v_t = [buf[:, n, :] for buf in (x_t, xb_t, y_t, z_t) for n in range(2)]
        w2_parts = w_hi[0:S3, 0, :]
        w2_f = z_t[0:S3, 0, :]
        w2_h = w_lo[0:S3, 1, :]
        w2_l = z_t[0:S3, 1, :]
        is_mid = y_t[0:S3, 0, D - 2:D]
        spare = yT[:].rearrange("p s c n -> p (s c n)")
        hid_t = spare[:, 0:2 * M2 * H].rearrange("p (s j c) -> p s j c", s=2, j=M2)
        agg_t = spare[:, 2 * M2 * H:4 * M2 * H].rearrange("p (s j c) -> p s j c", s=2, j=M2)
        sum33 = spare[:, 4 * M2 * H:4 * M2 * H + 2 * M2 * K2].rearrange("p (s j c) -> p s j c", s=2, j=M2)
        split = w_lo[:, 2:4, 0:M2 * S3].rearrange("p s (j h c) -> p s j h c", j=M2, h=3)
        splitT = zT_hi[0:S3, :, :, :]

        def gathered1(t):
            per = D // H
            return x_t[:, t // per, t % per * H:(t % per + 1) * H]

        edges_in = sem("edges_in")
        rows_in = sems("rows_in", 2)
        weights_in = sem("weights_in")
        small_in = sem("small_in")
        w2_in = sem("w2_in")
        iotas_done = sem("iotas_done")
        dve_seq = sem("dve_seq")
        dve_consts = sem("dve_consts")
        col_parts = sem("col_parts")
        keys_lowered = sem("keys_lowered")
        greater_made = sem("greater_made")
        compared = sem("compared")
        counted = sem("counted")
        placed_ready = sem("placed_ready")
        permuted = sem("permuted")
        edges_sorted = sem("edges_sorted")
        hist_ready = sem("hist_ready")
        hist_done = sem("hist_done")
        hist_taken = sem("hist_taken")
        prefix_ready = sem("prefix_ready")
        prefix_done = sem("prefix_done")
        ends_ready = sem("ends_ready")
        degree_ready = sem("degree_ready")
        degree_root = sem("degree_root")
        src_hot_ready = sem("src_hot_ready")
        dinv_ready = sem("dinv_ready")
        looked_up = sem("looked_up")
        weights_placed = sem("weights_placed")
        weights_permuted = sem("weights_permuted")
        edge_rows_in = [sems("edge_rows_in", ET), sems("edge_hid_in", ET)]
        key_row = sem("key_row")
        weights_taken = sem("weights_taken")
        w_split = sem("w_split")
        same_ready = sem("same_ready")
        tile_summed = sem("tile_summed")
        sum_copied = sem("sum_copied")
        sum_stored = sems("sum_stored", 2)
        x_in = sems("x_in", 2)
        end_prep = sem("end_prep")
        acc_in = sems("acc_in", 2)
        xb_done = sem("xb_done")
        z_done = sem("z_done")
        zT_done = sem("zT_done")
        hi_done = sem("hi_done")
        lo_done = sem("lo_done")
        prod_done = sem("prod_done")
        u_done = sem("u_done")
        stats_done = sem("stats_done")
        mv_done = sem("mv_done")
        sd_done = sem("sd_done")
        rstd_done = sem("rstd_done")
        shift_done = sem("shift_done")
        y_done = sem("y_done")
        y_kept = sems("y_kept", 2)
        yT_done = sem("yT_done")
        yT_copied = sem("yT_copied")
        pre_done = sem("pre_done")
        pre_taken = sem("pre_taken")
        r_done = sem("r_done")
        r_stored = sems("r_stored", 2)
        hid_in = sems("hid_in", 2)
        end_prep2 = sem("end_prep2")
        count_put = sem("count_put")
        agg_in = sems("agg_in", 2)
        add_done = sem("add_done")
        hi2_done = sem("hi2_done")
        split_done = sem("split_done")
        splitT_done = sem("splitT_done")
        splitT_copied = sem("splitT_copied")
        prod2_done = sem("prod2_done")
        v_done = sem("v_done")
        stats2_done = sem("stats2_done")
        mv2_done = sem("mv2_done")
        sd2_done = sem("sd2_done")
        rstd2_done = sem("rstd2_done")
        shift2_done = sem("shift2_done")
        out_done = sem("out_done")
        out_stored = sems("out_stored", 2 * M2)

        def key_rows(g, t):
            return psum[:, (0, t % 2)[g], 0:P]

        block = ctx.enter_context(nc.Block())

        def times(sem_list, k, t_before, m):
            return sem_list[k], 16 * (t_before + 1)

        @block.sync
        def _(sp):
            for g, a in enumerate((dst, src)):
                sp.dma_start(key_col_i[:, g, :], a.rearrange("(p t) -> p t", p=EP)).then_inc(edges_in, 16)
            sp.dma_start(ew_col, ew.rearrange("(p t) -> p t", p=EP)).then_inc(edges_in, 16)
            for g, a in enumerate((dst, src)):
                sp.dma_start(key_row_i[:, g, :], a.rearrange("(a e) -> a e", a=1).to_broadcast([P, E])).then_inc(rows_in[g], 16)
            sp.dma_start(w_f, w.rearrange("(c p) n -> p c n", p=P)).then_inc(weights_in, 16)
            sp.dma_start(bias[:], b.rearrange("(a n) -> a n", a=1).to_broadcast([P, D])).then_inc(small_in, 16)
            sp.dma_start(w1_sb[:], w1.rearrange("(c p) n -> p c n", p=P)).then_inc(small_in, 16)
            sp.dma_start(b1_sb[:], b1.rearrange("(a n) -> a n", a=1).to_broadcast([P, H])).then_inc(small_in, 16)

            def load_x(q, k):
                t = 2 * q + k
                wait(sp, z_done, t - 1)
                wait(sp, xb_done, t - 1)
                if isinstance(t, int) and t == NT - 1:
                    sp.dma_start(x_t[0:TAIL, k, :], x[t * P:N, :]).then_inc(x_in[k], 16)
                else:
                    sp.dma_start(x_t[:, k, :], x[bass.ds(t * P, P), :]).then_inc(x_in[k], 16)

            load_x(0, 0)
            load_x(0, 1)

            def store_sum(g, t):
                sp.wait_ge(sum_copied, g * ET + t + 1)
                dest, cols_ = ((sums0, D), (sums1, H))[g]
                sp.dma_start(dest[t * P:(t + 1) * P, :], sum_t[:, t % 2, 0:cols_]).then_inc(sum_stored[t % 2], 16)

            for t in range(ET):
                store_sum(0, t)

            def layer1_step(q, k):
                s = 2 * q + k
                static = isinstance(s, int)
                if not static or s + 2 < NT:
                    load_x(*before(q, k, -2, 2))
                if not static or 0 <= s - 2 < NT:
                    t, kk = s - 2, k
                    sp.wait_ge(y_done, t + 1)
                    sp.dma_start(Y[:, bass.ds(t * D, D)], y_t[:, kk, :]).then_inc(y_kept[kk], 16)
                if not static or 0 <= s - 4 < NT:
                    t, kk = s - 4, k
                    sp.wait_ge(r_done, t + 1)
                    if static and t == NT - 1:
                        sp.dma_start(hidden[t * P:N, :], r_t[0:TAIL, kk, :]).then_inc(r_stored[kk], 16)
                    else:
                        sp.dma_start(hidden[bass.ds(t * P, P), :], r_t[:, kk, :]).then_inc(r_stored[kk], 16)

            steps(sp, NT + 4, 6, 8, 2, layer1_step)

            sp.wait_ge(prod_done, NT)
            for c in range(3):
                sp.dma_start(w2_f[c * K2:c * K2 + H, :], w2).then_inc(w2_in, 16)
                sp.dma_start(w2_f[c * K2 + H:(c + 1) * K2, :], b2.rearrange("(a n) -> a n", a=1)).then_inc(w2_in, 16)

            for t in range(ET):
                store_sum(1, t)

            def load_hidden(q, k):
                g = 2 * q + k
                wait(sp, add_done, g - 1)
                if isinstance(g, int) and g == NG - 1:
                    for j in range(LAST):
                        t = g * M2 + j
                        n = TAIL if t == NT - 1 else P
                        sp.dma_start(hid_t[0:n, k, j, :], hidden[t * P:t * P + n, :]).then_inc(hid_in[k], 16)
                else:
                    sp.dma_start(hid_t[:, k, :, :], hidden[bass.ds(g * (M2 * P), M2 * P), :].rearrange(
                        "(j p) h -> p j h", p=P)).then_inc(hid_in[k], 16)

            for k in range(2):
                sp.wait_ge(r_stored[k], 16 * ((NT - k + 1) // 2))
            load_hidden(0, 0)
            load_hidden(0, 1)
            load_hidden(1, 0)

            def store_group(q, k):
                g = 2 * q + k
                static = isinstance(g, int)
                if not static or g + 3 < NG:
                    load_hidden(*before(q, k, -3, 2))
                for j in range(LAST if static and g == NG - 1 else M2):
                    t = g * M2 + j
                    n = k * M2 + j
                    sp.wait_ge(out_done, t + 1)
                    if static and t == NT - 1:
                        sp.dma_start(out[t * P:N, :], v_t[n][0:TAIL, :]).then_inc(out_stored[n], 16)
                    else:
                        sp.dma_start(out[bass.ds(t * P, P), :], v_t[n]).then_inc(out_stored[n], 16)

            steps(sp, NG, 2, 5, 2, store_group)
            for n in range(2 * M2):
                sp.wait_ge(out_stored[n], 16 * len(range(n, NT, 2 * M2)))

        @block.gpsimd
        def _(pool):
            pool.iota(iota_col, [[1, P]], base=0, channel_multiplier=0,
                      allow_small_or_imprecise_dtypes=True).then_inc(iotas_done, 1)
            pool.iota(iota_part[:], [[0, 1]], base=0, channel_multiplier=1,
                      allow_small_or_imprecise_dtypes=True).then_inc(iotas_done, 1)

            pool.wait_ge(col_parts, 1)
            for t in range(ET):
                pool.tensor_scalar(node_values[0:EP, t, 0, :], iota_col[0:EP, 0:NT], parts[0:EP, 0, 0, t:t + 1], None,
                                   ALU.is_equal)
                pool.tensor_scalar(node_values[0:EP, t, 1, :], iota_col[0:EP, 0:NT], parts[0:EP, 0, 0, t:t + 1],
                                   ew_col[:, t:t + 1], ALU.is_equal, ALU.mult)
                last = pool.tensor_scalar(node_lo[0][0:EP, t, :], iota_col[0:EP, 0:P], parts[0:EP, 1, 0, t:t + 1], None,
                                          ALU.is_equal)
            last.then_inc(hist_ready, 1)
            for t in range(ET):
                last = pool.tensor_scalar(src_hi[0:EP, t, :], iota_col[0:EP, 0:NT], parts[0:EP, 0, 1, t:t + 1], None,
                                          ALU.is_equal)
            for t in range(ET):
                last = pool.tensor_scalar(node_lo[1][0:EP, t, :], iota_col[0:EP, 0:P], parts[0:EP, 1, 1, t:t + 1], None,
                                          ALU.is_equal)
            last.then_inc(hist_ready, 1)

            pool.wait_ge(edges_sorted, 1)
            for t in range(ET):
                pool.indirect_dma_start(gathered[:, t, :], None, x,
                                        bass.IndirectOffsetOnAxis(ap=edge_row[:, 0, t:t + 1], axis=0),
                                        bounds_check=N - 1, oob_is_err=False).then_inc(edge_rows_in[0][t], 16)

            last_sum = pool.to_reg(ET * P - 1)

            def node_sums(q, k):
                t = 2 * q + k
                static = isinstance(t, int)
                if not static or t < NT:
                    wait(pool, zT_done, t - 1)
                    pool.tensor_copy(end_idx[:, k:k + 1], run_end[:, 0, bass.ds(t, 1)]).then_inc(end_prep, 1)
                    pool.memset(z_t[:, k, :], 0.0).then_inc(end_prep, 1)
                    pool.wait_ge(end_prep, 2 * t + 2)
                if not static or t >= 2:
                    pool.wait_ge(x_in[k], 16 * q)
                    wait(pool, u_done, t - 3)
                    pool.tensor_tensor(xb_t[:, k, :], x_t[:, k, :], bias[:], ALU.add).then_inc(xb_done, 1)
                if not static or t < NT:
                    pool.indirect_dma_start(z_t[:, k, :], None, sums0,
                                            bass.IndirectOffsetOnAxis(ap=end_idx[:, k:k + 1], axis=0),
                                            bounds_check=last_sum, oob_is_err=False).then_inc(acc_in[k], 16)

            for k in range(2):
                pool.wait_ge(sum_stored[k], 16 * (ET // 2))
            pool.wait_ge(ends_ready, 1)
            pool.wait_ge(small_in, 16 * 3)
            steps(pool, NT + 2, 4, 3, 2, node_sums)

            for k in range(2):
                pool.wait_ge(r_stored[k], 16 * ((NT - k + 1) // 2))
            for t in range(ET):
                pool.indirect_dma_start(gathered1(t), None, hidden,
                                        bass.IndirectOffsetOnAxis(ap=edge_row[:, 1, t:t + 1], axis=0),
                                        bounds_check=N - 1, oob_is_err=False).then_inc(edge_rows_in[1][t], 16)

            def node_sums2(q, k):
                g = 2 * q + k
                static = isinstance(g, int)
                wait(pool, add_done, g - 1)
                pool.tensor_copy(end_idx[:, k * M2:(k + 1) * M2], ends2[:, bass.ds(g * M2, M2)]).then_inc(end_prep2, 1)
                pool.memset(agg_t[:, k, :, :], 0.0).then_inc(end_prep2, 1)
                pool.wait_ge(end_prep2, 2 * g + 2)
                wait(pool, split_done, g - 1)
                pool.tensor_copy(sum33[:, k, :, H], fan[:, bass.ds(g * M2, M2)]).then_inc(count_put, 1)
                for j in range(LAST if static and g == NG - 1 else M2):
                    n = k * M2 + j
                    pool.indirect_dma_start(agg_t[:, k, j, :], None, sums1,
                                            bass.IndirectOffsetOnAxis(ap=end_idx[:, n:n + 1], axis=0),
                                            bounds_check=last_sum, oob_is_err=False).then_inc(agg_in[k], 16)

            for k in range(2):
                pool.wait_ge(sum_stored[k], 16 * ET)
            steps(pool, NG, 4, 2, 2, node_sums2)

        @block.scalar
        def _(act):
            act.wait_ge(degree_ready, 1)
            nc.scalar.activation(degree[:, 1, :], degree[:, 1, :], ACT.Sqrt).then_inc(degree_root, 1)

            def copy_sum(g, t):
                act.wait_ge(tile_summed, g * ET + t + 1)
                n = g * (ET // 2) + t // 2
                wait(act, sum_stored[t % 2], 16 * n)
                c = (D, H)[g]
                nc.scalar.copy(sum_t[:, t % 2, 0:c], psum[:, 6 + t % 2, 0:c]).then_inc(sum_copied, 1)

            for t in range(ET):
                copy_sum(0, t)

            def layer1_step(q, k):
                s = 2 * q + k
                static = isinstance(s, int)
                if not static or s < NT:
                    act.wait_ge(zT_done, s + 1)
                    wait(act, prod_done, s - 1)
                    nc.scalar.copy(zT_hi[:, k, :, :].rearrange("p c n -> p (c n)"), psum[:, k, :]).then_inc(hi_done, 1)
                if not static or 0 <= s - 3 < NT:
                    t, kk = s - 3, (k - 3) % 2
                    act.wait_ge(yT_done, t + 1)
                    wait(act, pre_done, t - 1)
                    nc.scalar.copy(yT[:, kk, :, :].rearrange("p c n -> p (c n)"), psum[:, 4 + kk, :]).then_inc(yT_copied, 1)
                if not static or 0 <= s - 4 < NT:
                    t, kk = s - 4, k
                    act.wait_ge(pre_taken, t + 1)
                    nc.scalar.activation(r_t[:, kk, :], r_t[:, kk, :], ACT.Relu).then_inc(r_done, 1)
                if not static or 0 <= s - 2 < NT:
                    t, kk = s - 2, k
                    act.wait_ge(mv_done, t + 1)
                    nc.scalar.activation(sd[:, kk:kk + 1], mv[:, kk, 1:2], ACT.Sqrt, bias=eps[:, 0:1]).then_inc(sd_done, 1)
                    act.wait_ge(shift_done, t + 1)
                    nc.scalar.activation(y_t[:, kk, :], y_t[:, kk, :], ACT.Identity, bias=shift[:, kk:kk + 1],
                                         scale=rstd[:, kk:kk + 1]).then_inc(y_done, 1)

            steps(act, NT + 4, 6, 5, 2, layer1_step)

            for t in range(ET):
                copy_sum(1, t)

            def copy_splits(q, k):
                g = 2 * q + k
                act.wait_ge(splitT_done, g + 1)
                wait(act, prod2_done, (g - 1) * M2)
                nc.scalar.copy(splitT[:, k, :, :].rearrange("p c n -> p (c n)"), psum[0:S3, 4 + k, :]).then_inc(splitT_copied, 1)

            def layer2_group(q, k):
                g = 2 * q + k
                static = isinstance(g, int)
                has_next = not static or g + 1 < NG
                if static and g == 0:
                    copy_splits(q, k)
                if not static or g - 1 >= 0:
                    kk = 1 - k
                    tiles = LAST if static and g == NG else M2
                    these = slice(kk * M2, (kk + 1) * M2)
                    act.wait_ge(mv2_done, (g - 1) * M2 + tiles)
                    nc.scalar.activation(sd[:, these], mv[:, these, 1], ACT.Sqrt, bias=eps[:, 0:1]).then_inc(sd2_done, 1)
                    act.wait_ge(shift2_done, g)
                    for j in range(tiles):
                        if j == 2 and has_next:
                            copy_splits(*before(q, k, -1, 2))
                        n = kk * M2 + j
                        nc.scalar.activation(v_t[n], v_t[n], ACT.Identity, bias=shift[:, n:n + 1],
                                             scale=rstd[:, n:n + 1]).then_inc(out_done, 1)
                elif has_next:
                    copy_splits(*before(q, k, -1, 2))

            steps(act, NG + 1, 4, 3, 2, layer2_group)

        @block.vector
        def _(dve):
            seq = [0]

            def then(ins):
                seq[0] += 1
                ins.then_inc(dve_seq, 1)
                dve.wait_ge(dve_seq, seq[0])

            dve.memset(ones, 1.0)
            dve.memset(eps[:], EPS)
            dve.memset(ones16, 1.0)
            dve.memset(fan[:], 1.0)
            dve.memset(run_end[:, 1, NT:NT + 1], 0)
            dve.wait_ge(iotas_done, 2)
            dve.tensor_scalar(ident[:], iota_col, iota_part[:, 0:1], None, ALU.is_equal)
            dve.tensor_scalar(below, iota_col, iota_part[:, 0:1], None, ALU.is_gt)
            then(dve.tensor_scalar(last_row[:], iota_part[:], float(P - 1), None, ALU.is_equal))
            dve.memset(prev_key[:], 0.0).then_inc(dve_consts, 1)
            dve.wait_ge(edges_in, 48)
            dve.tensor_copy(cols, key_col_i)
            dve.tensor_scalar(ints[0:EP, 1], key_col_i, P - 1, None, ALU.bitwise_and)
            then(dve.tensor_scalar(ints[0:EP, 0], key_col_i, 7, None, ALU.logical_shift_right))
            dve.tensor_copy(parts[0:EP], ints[0:EP]).then_inc(col_parts, 1)
            dve.tensor_copy(parts16[0:EP], ints[0:EP].rearrange("p h g t -> p (h g) t"))
            dve.tensor_copy(iota16, iota_col)

            def widen_keys(g):
                if g == 1:
                    dve.wait_ge(compared, ET)
                dve.tensor_scalar(twice, cols[:, g, :], 2.0, None, ALU.mult)
                dve.wait_ge(rows_in[g], 16)
                row = row_keys.rearrange("q (t p) -> q t p", t=ET)
                then(dve.tensor_scalar(row, key_row_i[:, g, :].rearrange("q (p t) -> q t p", t=ET),
                                       2.0, 1.0, ALU.mult, ALU.add))

            def compare(g, q, k):
                t = PER * q + k
                n = g * ET + t
                here = row_keys[0:EP, bass.ds(t * EP, EP)]
                wait(dve, greater_made, n)
                dve.tensor_scalar(here, here, 1.0, None, ALU.subtract).then_inc(keys_lowered, 1)
                dve.wait_ge(keys_lowered, n + 1)
                wait(dve, counted, n - 1)
                dve.tensor_scalar(greater[0:EP, k % 2, :], row_keys[0:EP, :], twice[:, bass.ds(t, 1)], None,
                                  ALU.is_gt).then_inc(greater_made, 1)
                dve.scalar_tensor_tensor(tied[0:EP, k % 2, 0:EP], here, twice[:, bass.ds(t, 1)], below[0:EP, 0:EP],
                                         ALU.is_equal, ALU.mult).then_inc(compared, 1)

            def place_edges(g):
                dve.wait_ge(counted, (g + 1) * ET)
                for t in range(ET):
                    last = dve.scalar_tensor_tensor(diagonal[:, t, :], psum[0:EP, 1 + t // PER, t % PER * EP:(t % PER + 1) * EP],
                                                    1.0, ident[0:EP, 0:EP], ALU.mult, ALU.mult, accum_out=ranks[0:EP, t:t + 1])
                then(last)
                then(dve.tensor_copy(rank_ints[0:EP, 0, :], ranks[0:EP, :]))
                dve.tensor_scalar(rank_ints[0:EP, 1, :], rank_ints[0:EP, 0, :], P - 1, None, ALU.bitwise_and)
                then(dve.tensor_scalar(rank_ints[0:EP, 0, :], rank_ints[0:EP, 0, :], 7, None, ALU.logical_shift_right))
                then(dve.tensor_copy(rank_parts[0:EP], rank_ints[0:EP]))
                then(dve.tensor_tensor(hot_hi[0:EP], iota16[0:EP, None, 0:ET].to_broadcast([EP, ET, ET]),
                                       rank_parts[0:EP, 0, :, None].to_broadcast([EP, ET, ET]), ALU.is_equal))
                dve.tensor_tensor(placed[0:EP, :, 0:4, :], hot_hi[0:EP, :, None, :].to_broadcast([EP, ET, 4, ET]),
                                  parts16[0:EP].rearrange("p v t -> p t v")[:, :, :, None].to_broadcast([EP, ET, 4, ET]), ALU.mult)
                if g == 1:
                    dve.tensor_copy(placed[0:EP, :, 4, :], hot_hi[0:EP])
                dve.tensor_tensor(hot_lo[0:EP], iota16[0:EP, None, 0:P].to_broadcast([EP, ET, P]),
                                  rank_parts[0:EP, 1, :, None].to_broadcast([EP, ET, P]), ALU.is_equal).then_inc(placed_ready, 1)

            def take_sorted(g):
                dve.wait_ge(permuted, g + 1)
                if g == 1:
                    dve.tensor_copy(edge[:, 1, 2, :], psum[:, 6, 4 * ET:5 * ET])
                then(dve.tensor_copy(sorted_parts.rearrange("p h g t -> p (h g t)"), psum[:, 6, 0:4 * ET]))
                for v, side in enumerate((g, 1 - g)):
                    last = dve.scalar_tensor_tensor(edge[:, g, v, :], sorted_parts[:, 0, side, :], float(P),
                                                    sorted_parts[:, 1, side, :], ALU.mult, ALU.add)
                then(last)
                dve.tensor_copy(edge_row[:, g, :], edge[:, g, 1, :]).then_inc(edges_sorted, 1)

            def split_in_three(to, values, rest_):
                then(dve.tensor_copy(to[0], values))
                then(dve.tensor_tensor(rest_, values, to[0], ALU.subtract))
                then(dve.tensor_copy(to[1], rest_))
                return dve.tensor_tensor(to[2], rest_, to[1], ALU.subtract)

            def src_one_hots():
                dve.wait_ge(rows_in[1], 16)
                then(dve.tensor_scalar(row_lo.rearrange("q (t p) -> q t p", t=ET),
                                       key_row_i[:, 1, :].rearrange("q (p t) -> q t p", t=ET),
                                       P - 1, None, ALU.bitwise_and))
                dve.tensor_scalar(src_hot, row_lo, iota_part[:, 0:1], None, ALU.is_equal).then_inc(src_hot_ready, 1)

            def take_degree():
                dve.wait_ge(hist_done, 1)
                dve.tensor_copy(count_[:, 0, :], psum[:, 7, 0:NT])
                then(dve.tensor_scalar(degree[:, 0, :], psum[:, 7, NT:2 * NT], 1.0, None, ALU.add))
                dve.tensor_scalar(degree[:, 1, :], degree[:, 0, :], SMALLEST_DEGREE, None, ALU.max).then_inc(degree_ready, 1)
                dve.tensor_scalar(half, degree[:, 0, :], SMALLEST_DEGREE, -0.5, ALU.max, ALU.mult).then_inc(hist_taken, 1)

            def take_dinv():
                dve.wait_ge(degree_root, 1)
                then(dve.reciprocal(guess, degree[:, 1, :]))
                then(dve.tensor_tensor(half, half, guess, ALU.mult))
                then(dve.tensor_tensor(half, half, guess, ALU.mult))
                then(dve.scalar_tensor_tensor(guess, half, 1.5, guess, ALU.add, ALU.mult))
                then(dve.scalar_tensor_tensor(dinv[:], degree[:, 0, :], 0.0, guess, ALU.is_gt, ALU.mult))
                split_in_three([dinv_parts[:, v, :] for v in range(3)], dinv[:], rest).then_inc(dinv_ready, 1)

            def count_before():
                dve.wait_ge(hist_done, 2)
                then(dve.tensor_copy(count_[:, 1, :], psum[:, 5, 0:NT]))
                dve.memset(flat[:, 0, :, 0:1], 0.0)
                dve.tensor_scalar(fan[:, 0:NT], count_[:, 1, :], 1.0, None, ALU.add)
                then(dve.tensor_copy(flat[:, 0, :, 1:NT], count_[:, :, 0:NT - 1]))
                at, width = 0, 1
                while width < NT:
                    dve.tensor_copy(flat[:, 1 - at, :, 0:width], flat[:, at, :, 0:width])
                    then(dve.tensor_tensor(flat[:, 1 - at, :, width:NT], flat[:, at, :, width:NT],
                                           flat[:, at, :, 0:NT - width], ALU.add))
                    at, width = 1 - at, 2 * width
                assert at == 1
                dve.tensor_scalar(flat[:, 0], count_, 0.0, NO_ROW, ALU.is_equal, ALU.mult).then_inc(prefix_ready, 1)

            def take_ends():
                dve.wait_ge(prefix_done, 1)
                dve.wait_ge(prefix_ready, 1)
                dve.scalar_tensor_tensor(run_end[:, :, 0:NT], psum[:, 0, 0:2 * NT].rearrange("p (g c) -> p g c", g=2), -1.0,
                                         flat[:, 0], ALU.add, ALU.add).then_inc(ends_ready, 1)

            def weigh_edges():
                for n, t in enumerate(range(0, ET, LOOKS)):
                    tiles = min(LOOKS, ET - t)
                    dve.wait_ge(looked_up, n + 1)
                    last = dve.tensor_tensor(look_prod[0:EP, t:t + tiles, :],
                                             psum[0:EP, 1 + n, 0:tiles * NT].rearrange("p (t c) -> p t c", t=tiles),
                                             src_hi[0:EP, t:t + tiles, :], ALU.mult)
                then(last)
                then(dve.tensor_reduce(src_inv[0:EP, :], look_prod[0:EP], AXIS.X, ALU.add))
                then(dve.tensor_tensor(src_inv[0:EP, :], src_inv[0:EP, :], ew_col, ALU.mult))
                then(split_in_three([weight_parts[0:EP, v, :] for v in range(3)], src_inv[0:EP, :], rest[0:EP, 0:ET]))
                dve.tensor_tensor(placed_weights[0:EP], hot_hi[0:EP, :, None, :].to_broadcast([EP, ET, 3, ET]),
                                  weight_parts[0:EP].rearrange("p v t -> p t v")[:, :, :, None].to_broadcast([EP, ET, 3, ET]),
                                  ALU.mult).then_inc(weights_placed, 1)

            def match_keys(g, t):
                k, n = t % 2, g * ET + t
                dve.wait_ge(key_row, n + 1)
                wait(dve, tile_summed, n - 1)
                wait(dve, same_ready, n)
                row = key_rows(g, t)
                dve.tensor_scalar(same[:, k, :], row, edge[:, g, 0, t:t + 1], edge[:, g, 2, t:t + 1],
                                  ALU.is_equal, ALU.mult)
                if t > 0:
                    dve.tensor_scalar(open_run[:, k, :], row, prev_key[:, 1 - k:2 - k], last_row[:, 0:1],
                                      ALU.is_equal, ALU.mult)
                dve.tensor_copy(prev_key[:, k:k + 1], row[:, P - 1:P]).then_inc(same_ready, 1)

            widen_keys(0)
            steps(dve, ET, PER, 0, PER, lambda q, k: compare(0, q, k))
            src_one_hots()
            place_edges(0)
            take_degree()
            take_sorted(0)
            take_dinv()
            count_before()
            widen_keys(1)
            weigh_edges()
            take_ends()
            dve.wait_ge(weights_permuted, 1)
            dve.tensor_reduce(edge[:, 0, 2, :], psum[:, 7, 0:3 * ET].rearrange("p (v t) -> p t v", v=3), AXIS.X,
                              ALU.add).then_inc(weights_taken, 1)
            dve.wait_ge(weights_taken, 1)
            match_keys(0, 0)
            for t in range(ET):
                compare(1, t // PER, t % PER)
                if t + 1 < ET:
                    match_keys(0, t + 1)
            dve.wait_ge(weights_in, 16)
            then(dve.tensor_copy(w_hi[:], w_f))
            dve.tensor_tensor(w_lo[:], w_f, w_hi[:].bitcast(F32), ALU.subtract).then_inc(w_split, 1)
            place_edges(1)
            take_sorted(1)

            def make_z(q, k):
                dve.wait_ge(x_in[k], 16 * (q + 1))
                dve.wait_ge(acc_in[k], 16 * (q + 1))
                t = 2 * q + k
                dve.scalar_tensor_tensor(z_t[:, k, :], x_t[:, k, :], dinv[:, bass.ds(t, 1)], z_t[:, k, :],
                                         ALU.mult, ALU.add).then_inc(z_done, 1)

            make_z(0, 0)

            def layer1_step(q, k):
                s = 2 * q + k
                static = isinstance(s, int)
                has_u = not static or 0 <= s - 2 < NT
                t, kk = s - 2, k
                if has_u:
                    dve.wait_ge(prod_done, t + 1)
                    dve.wait_ge(xb_done, t + 1)
                    wait(dve, yT_done, t - 1)
                    wait(dve, y_kept[kk], 16 * (q - 1))
                    dve.scalar_tensor_tensor(y_t[:, kk, :], psum[:, 2 + kk, :], dinv[:, bass.ds(t, 1)], xb_t[:, kk, :],
                                             ALU.mult, ALU.add).then_inc(u_done, 1)
                    dve.wait_ge(u_done, t + 1)
                    dve.bn_stats(stats[:, kk, :], y_t[:, kk, :]).then_inc(stats_done, 1)
                    dve.wait_ge(iotas_done, 2)
                    dve.wait_ge(stats_done, t + 1)
                    dve.bn_aggr(mv[:, kk, :], stats[:, kk, :]).then_inc(mv_done, 1)
                if not static or s < NT:
                    dve.wait_ge(hi_done, s + 1)
                    wait(dve, prod_done, s - 1)
                    dve.tensor_tensor(zT_lo[:, k, :, :].rearrange("p c n -> p (c n)"), psum[:, k, :],
                                      zT_hi[:, k, :, :].rearrange("p c n -> p (c n)").bitcast(F32),
                                      ALU.subtract).then_inc(lo_done, 1)
                if not static or 0 <= s - 4 < NT:
                    dve.wait_ge(pre_done, s - 3)
                    wait(dve, r_stored[k], 16 * (q - 2))
                    dve.tensor_tensor(r_t[:, k, :], psum[:, 6 + k, 0:H], b1_sb[:], ALU.add).then_inc(pre_taken, 1)
                if has_u:
                    dve.wait_ge(sd_done, t + 1)
                    wait(dve, y_done, t - 1)
                    dve.reciprocal(rstd[:, kk:kk + 1], sd[:, kk:kk + 1]).then_inc(rstd_done, 1)
                    dve.wait_ge(rstd_done, t + 1)
                    dve.scalar_tensor_tensor(shift[:, kk:kk + 1], mv[:, kk, 0:1], -1.0, rstd[:, kk:kk + 1],
                                             ALU.mult, ALU.mult).then_inc(shift_done, 1)
                if not static or s + 1 < NT:
                    make_z(*before(q, k, -1, 2))

            steps(dve, NT + 4, 6, 5, 2, layer1_step)

            dve.wait_ge(prod_done, NT)
            for t in range(ET):
                match_keys(1, t)
            dve.wait_ge(w2_in, 16 * 6)
            then(dve.tensor_copy(w2_h, w2_f))
            dve.tensor_scalar(is_mid[:, 0:1], iota_part[0:S3, :], float(K2), None, ALU.is_ge)
            then(dve.tensor_scalar(is_mid[:, 1:2], iota_part[0:S3, :], float(2 * K2), None, ALU.is_lt))
            then(dve.tensor_tensor(is_mid[:, 0:1], is_mid[:, 0:1], is_mid[:, 1:2], ALU.mult))
            then(dve.tensor_scalar(is_mid[:, 1:2], is_mid[:, 0:1], -1.0, 1.0, ALU.mult, ALU.add))
            then(dve.tensor_tensor(w2_l, w2_f, w2_h.bitcast(F32), ALU.subtract))
            then(dve.tensor_scalar(w2_l, w2_l, is_mid[:, 0:1], None, ALU.mult))
            then(dve.scalar_tensor_tensor(w2_parts, w2_h.bitcast(F32), is_mid[:, 1:2], w2_l, ALU.mult, ALU.add))

            def add_sums(q, k):
                g = 2 * q + k
                static = isinstance(g, int)
                if static and g == NG - 1:
                    dve.wait_ge(hid_in[k], 16 * (q + LAST))
                    dve.wait_ge(agg_in[k], 16 * (q * M2 + LAST))
                else:
                    dve.wait_ge(hid_in[k], 16 * (q + 1))
                    dve.wait_ge(agg_in[k], 16 * M2 * (q + 1))
                wait(dve, split_done, g - 1)
                dve.tensor_tensor(sum33[:, k, :, 0:H], hid_t[:, k, :, :], agg_t[:, k, :, :], ALU.add).then_inc(add_done, 1)

            def split_hi(q, k):
                g = 2 * q + k
                dve.wait_ge(add_done, g + 1)
                dve.wait_ge(count_put, g + 1)
                wait(dve, splitT_done, g - 1)
                dve.tensor_copy(split[:, k, :, 0:2, :],
                                sum33[:, k, :, None, :].to_broadcast([P, M2, 2, K2])).then_inc(hi2_done, 1)

            def split_lo(q, k):
                g = 2 * q + k
                dve.wait_ge(hi2_done, g + 1)
                dve.tensor_tensor(split[:, k, :, 2, :], sum33[:, k, :, :], split[:, k, :, 0, :].bitcast(F32),
                                  ALU.subtract).then_inc(split_done, 1)

            for part in (add_sums, split_hi, split_lo):
                part(0, 0)

            def layer2_group(q, k):
                g = 2 * q + k
                static = isinstance(g, int)
                tiles = 0 if static and g >= NG else LAST if static and g == NG - 1 else M2

                def make_v(j):
                    if j < tiles:
                        t, n = g * M2 + j, k * M2 + j
                        dve.wait_ge(prod2_done, t + 1)
                        wait(dve, out_stored[n], 16 * q)
                        dve.tensor_tensor(v_t[n], psum[:, j, :], Y[:, bass.ds(t * D, D)], ALU.add).then_inc(v_done, 1)

                def take_stats(j):
                    if 0 <= j < tiles:
                        t, n = g * M2 + j, k * M2 + j
                        dve.wait_ge(v_done, t + 1)
                        dve.bn_stats(stats[:, n, :], v_t[n]).then_inc(stats2_done, 1)

                def take_mv(j):
                    if 0 <= j < tiles:
                        t, n = g * M2 + j, k * M2 + j
                        dve.wait_ge(iotas_done, 2)
                        dve.wait_ge(stats2_done, t + 1)
                        dve.bn_aggr(mv[:, n, :], stats[:, n, :]).then_inc(mv2_done, 1)

                last = slice((1 - k) * M2, (2 - k) * M2)
                has_last = not static or 0 <= g - 1 < NG
                has_next = not static or g + 1 < NG
                make_v(0)
                if has_next:
                    add_sums(*before(q, k, -1, 2))
                if has_last:
                    dve.wait_ge(sd2_done, g)
                    wait(dve, out_done, (g - 2) * M2)
                    dve.reciprocal(rstd[:, last], sd[:, last]).then_inc(rstd2_done, 1)
                make_v(1)
                if has_next:
                    split_hi(*before(q, k, -1, 2))
                if has_last:
                    dve.wait_ge(rstd2_done, g)
                    dve.scalar_tensor_tensor(shift[:, last], mv[:, last, 0], -1.0, rstd[:, last],
                                             ALU.mult, ALU.mult).then_inc(shift2_done, 1)
                take_stats(0)
                if has_next:
                    split_lo(*before(q, k, -1, 2))
                make_v(2)
                take_mv(0)
                take_stats(1)
                make_v(3)
                take_mv(1)
                take_stats(2)
                take_stats(3)
                take_mv(2)
                take_mv(3)

            steps(dve, NG + 1, 4, 3, 2, layer2_group)

        @block.tensor
        def _(pe):
            pe.wait_ge(dve_consts, 1)

            def count(g, q, k):
                t = PER * q + k
                pe.wait_ge(compared, g * ET + t + 1)
                for c in range(CHUNKS):
                    pe.matmul(psum[0:EP, 1 + c, 0:CHUNK], ones16[0:EP, 0:EP], greater[0:EP, k % 2, c * CHUNK:(c + 1) * CHUNK],
                              start=isinstance(t, int) and t == 0, stop=False, skip_group_check=True)
                pe.matmul(psum[0:EP, 1 + q, k * EP:(k + 1) * EP], ones16[0:EP, 0:EP], tied[0:EP, k % 2, 0:EP],
                          start=False, stop=False, skip_group_check=True).then_inc(counted, 1)

            def permute(g):
                pe.wait_ge(placed_ready, g + 1)
                for t in range(ET):
                    mm = pe.matmul(psum[:, 6, 0:(4 + g) * ET], hot_lo[0:EP, t, :],
                                   placed[0:EP, t, 0:4 + g, :].rearrange("p v c -> p (v c)"), start=t == 0, stop=t == ET - 1)
                mm.then_inc(permuted, 1)

            def row_of(out_ap, column):
                return pe.matmul(out_ap, column.to_broadcast([P, P]), ident[:], start=True, stop=True)

            def sum_tile(g, t, between=None):
                c = (D, H)[g]
                k, n = t % 2, g * ET + t
                if g == 0:
                    pe.wait_ge(same_ready, n + 1)
                if t + 1 < ET:
                    wait(pe, same_ready, n)
                    row_of(key_rows(g, t + 1), edge[:, g, 0, t + 1:t + 2]).then_inc(key_row, 1)
                if g == 1:
                    pe.wait_ge(same_ready, n + 1)
                pe.wait_ge(edge_rows_in[g][t], 16)
                wait(pe, sum_copied, n - 1)
                rows = gathered[:, t, :] if g == 0 else gathered1(t)
                mm = pe.matmul(psum[:, 6 + k, 0:c], same[:, k, :], rows, start=True, stop=t == 0)
                if t == 0:
                    mm.then_inc(tile_summed, 1)
                if between:
                    between()
                if t > 0:
                    pe.wait_ge(sum_copied, n)
                    pe.matmul(psum[:, 6 + k, 0:c], open_run[:, k, :], sum_t[:, 1 - k, 0:c], start=False,
                              stop=True).then_inc(tile_summed, 1)

            steps(pe, ET, PER, 0, PER, lambda q, k: count(0, q, k))
            pe.wait_ge(hist_ready, 1)
            for t in range(ET):
                mm = pe.matmul(psum[:, 7, 0:2 * NT], node_lo[0][0:EP, t, :],
                               node_values[0:EP, t, :, :].rearrange("p v c -> p (v c)"), start=t == 0, stop=t == ET - 1)
            mm.then_inc(hist_done, 1)
            permute(0)
            pe.wait_ge(hist_ready, 2)
            for t in range(ET):
                mm = pe.matmul(psum[:, 5, 0:NT], node_lo[1][0:EP, t, :], src_hi[0:EP, t, :], start=t == 0, stop=t == ET - 1)
            mm.then_inc(hist_done, 1)
            pe.wait_ge(src_hot_ready, 1)
            pe.wait_ge(dinv_ready, 1)
            for t in range(ET):
                for v in range(3):
                    mm = pe.matmul(psum[0:EP, 1 + t // LOOKS, t % LOOKS * NT:(t % LOOKS + 1) * NT],
                                   src_hot[:, t * EP:(t + 1) * EP], dinv_parts[:, v, :], start=v == 0, stop=v == 2)
                if t % LOOKS == LOOKS - 1 or t == ET - 1:
                    mm.then_inc(looked_up, 1)
            pe.wait_ge(prefix_ready, 1)
            ends = psum[:, 0, 0:2 * NT]
            pe.matmul(ends, ones, flat[:, 1].rearrange("p g c -> p (g c)"), start=True, stop=False)
            pe.matmul(ends, below, count_.rearrange("p g c -> p (g c)"), start=False, stop=False)
            pe.matmul(ends, ident[:], count_.rearrange("p g c -> p (g c)"), start=False, stop=True).then_inc(prefix_done, 1)
            pe.wait_ge(hist_taken, 1)
            pe.wait_ge(weights_placed, 1)
            for t in range(ET):
                mm = pe.matmul(psum[:, 7, 0:3 * ET], hot_lo[0:EP, t, :],
                               placed_weights[0:EP, t, :, :].rearrange("p v c -> p (v c)"), start=t == 0, stop=t == ET - 1)
            mm.then_inc(weights_permuted, 1)

            pe.wait_ge(ends_ready, 1)
            pe.wait_ge(edges_sorted, 1)
            row_of(key_rows(0, 0), edge[:, 0, 0, 0:1]).then_inc(key_row, 1)
            for t in range(ET):
                sum_tile(0, t, lambda: count(1, t // PER, t % PER))
            permute(1)

            def layer1_step(q, k):
                s = 2 * q + k
                static = isinstance(s, int)
                if not static or s < NT:
                    pe.wait_ge(z_done, s + 1)
                    wait(pe, hi_done, s - 1)
                    wait(pe, lo_done, s - 1)
                    for c in range(KC):
                        mm = pe.transpose(psum[:, k, c * P:(c + 1) * P], z_t[:, k, c * P:(c + 1) * P], ident[:])
                    mm.then_inc(zT_done, 1)
                if not static or 0 <= s - 3 < NT:
                    t, kk = s - 3, (k - 3) % 2
                    pe.wait_ge(y_done, t + 1)
                    wait(pe, yT_copied, t - 1)
                    for c in range(KC):
                        mm = pe.transpose(psum[:, 4 + kk, c * P:(c + 1) * P], y_t[:, kk, c * P:(c + 1) * P], ident[:])
                    mm.then_inc(yT_done, 1)
                if not static or 0 <= s - 1 < NT:
                    t, kk = s - 1, (k - 1) % 2
                    pe.wait_ge(hi_done, t + 1)
                    pe.wait_ge(lo_done, t + 1)
                    wait(pe, u_done, t - 1)
                    n = 0
                    for c in range(KC):
                        for a, bb in ((zT_hi, w_hi), (zT_hi, w_lo), (zT_lo, w_hi)):
                            mm = pe.matmul(psum[:, 2 + kk, :], a[:, kk, c, :], bb[:, c, :], start=n == 0, stop=n == 3 * KC - 1)
                            n += 1
                    mm.then_inc(prod_done, 1)
                if not static or 0 <= s - 3 < NT:
                    t, kk = s - 3, (k - 3) % 2
                    pe.wait_ge(yT_copied, t + 1)
                    wait(pe, pre_taken, t - 1)
                    pre = psum[:, 6 + kk, 0:H]
                    for c in range(KC):
                        mm = pe.matmul(pre, yT[:, kk, c, :], w1_sb[:, c, :], start=c == 0, stop=c == KC - 1)
                    mm.then_inc(pre_done, 1)

            pe.wait_ge(w_split, 1)
            pe.wait_ge(small_in, 16 * 3)
            steps(pe, NT + 4, 6, 5, 2, layer1_step)

            row_of(key_rows(1, 0), edge[:, 1, 0, 0:1]).then_inc(key_row, 1)
            for t in range(ET):
                sum_tile(1, t)

            def transpose_splits(q, k):
                g = 2 * q + k
                pe.wait_ge(split_done, g + 1)
                wait(pe, splitT_copied, g - 1)
                for j in range(M2):
                    mm = pe.transpose(psum[0:S3, 4 + k, j * P:(j + 1) * P],
                                      split[:, k, j, :, :].rearrange("p h c -> p (h c)").bitcast(F32), ident[:])
                mm.then_inc(splitT_done, 1)

            def layer2_group(q, k):
                g = 2 * q + k
                static = isinstance(g, int)
                if static and g == 0:
                    transpose_splits(q, k)
                pe.wait_ge(splitT_copied, g + 1)
                for j in range(LAST if static and g == NG - 1 else M2):
                    wait(pe, v_done, (g - 1) * M2 + j + 1)
                    pe.matmul(psum[:, j, :], splitT[:, k, j, :], w2_parts, start=True, stop=True).then_inc(prod2_done, 1)
                if not static or g + 1 < NG:
                    transpose_splits(*before(q, k, -1, 2))

            steps(pe, NG, 4, 2, 2, layer2_group)


_INS = ['x', 'src', 'dst', 'edge_weight', 'L0_gnn_W', 'L0_gnn_b', 'L1_gnn_W1', 'L1_gnn_b1', 'L1_gnn_W2', 'L1_gnn_b2']


def kernel(**inputs):
    import numpy as _np
    import concourse.bacc as _bacc
    from concourse import mybir as _mybir
    from concourse.bass_utils import run_bass_kernel_spmd as _run

    nc = _bacc.Bacc("TRN2", target_bir_lowering=False, num_devices=1)
    arrays, args = {}, []
    for name in _INS:
        a = _np.ascontiguousarray(inputs[name])
        arrays[f"in_{name}_dram"] = a
        args.append(nc.dram_tensor(f"in_{name}_dram", a.shape, _mybir.dt.from_np(a.dtype), kind="ExternalInput").ap())
    out = nc.dram_tensor("out_0_dram", inputs["x"].shape, _mybir.dt.float32, kind="ExternalOutput").ap()
    graph_layers(nc, *args, out)
    r = _run(nc, [arrays], core_ids=[0])
    return r.results[0]["out_0_dram"]
```

```python
from contextlib import ExitStack

import concourse.bass as bass
from concourse import mybir

F32 = mybir.dt.float32
F32R = mybir.dt.float32r
BF16 = mybir.dt.bfloat16
I32 = mybir.dt.int32
I16 = mybir.dt.int16
ALU = mybir.AluOpType
ACT = mybir.ActivationFunctionType
AXIS = mybir.AxisListType

P = 128
EPS = 1e-5
SMALLEST_DEGREE = 1e-30
NO_ROW = 8192.0


def before(q, k, n, m):
    return q + (k - n) // m, (k - n) % m


def wait(eng, sem, value):
    if not isinstance(value, int) or value > 0:
        eng.wait_ge(sem, value)


def steps(eng, total, head, tail, m, step):
    assert head % m == 0
    rounds = (total - head - tail) // m
    for s in range(head):
        step(s // m, s % m)
    with eng.Fori(0, rounds) as r:
        for k in range(m):
            step(r + head // m, k)
    for s in range(head + rounds * m, total):
        step(s // m, s % m)


def in_fours(step):
    return lambda q, k: step(2 * q + k // 2, k % 2)


def graph_layers(nc, x, src, dst, ew, w, b, w1, b1, w2, b2, out):
    N, D = x.shape
    E = src.shape[0]
    H = w1.shape[1]
    KC = D // P
    NT = -(-N // P)
    TAIL = N - (NT - 1) * P
    ET = -(-E // P)
    EP = E // ET
    assert EP * ET == E and EP <= P and D == KC * P
    assert 2 * N + 1 < 1 << 15 and NT <= P
    ACT_FROM, ACT_TO = 3 * ET // 10, 7 * ET // 10
    DVE_TILES = [t for t in range(ET) if not ACT_FROM <= t < ACT_TO]
    ND = len(DVE_TILES)
    NA = ET - ND
    assert ACT_FROM > 0 and ACT_TO < ET
    LOOKS = 512 // NT
    K2 = H + 1
    S3 = 3 * K2

    sums0 = nc.dram_tensor("edge_sums_0", (ET * P, D), F32).ap()
    sums1 = nc.dram_tensor("edge_sums_1", (ET * P, H), F32).ap()
    hidden = nc.dram_tensor("hidden", (N, H), F32).ap()

    with ExitStack() as ctx:
        def sb(name, shape, dt=F32):
            return ctx.enter_context(nc.sbuf_tensor(name, shape, dt))

        def sem(name):
            return ctx.enter_context(nc.semaphore(name))

        def sems(name, n):
            return [sem(f"{name}{i}") for i in range(n)]

        Y = sb("Y", [P, NT * D])
        taken = [0]

        def scratch(words):
            at = taken[0]
            taken[0] += words
            assert taken[0] <= NT * D
            return Y[:, at:at + words]

        key_row_i = scratch(2 * E).bitcast(I32).rearrange("p (g e) -> p g e", g=2)
        assert taken[0] >= 6 * D
        iota_col = scratch(P)
        iota_part = sb("iota_part", [P, 1])
        ident = sb("ident", [P, P])
        below = scratch(P)
        last_row = sb("last_row", [P, 1])
        ones = scratch(P)
        eps = sb("eps", [P, 1])
        bias = sb("bias", [P, D])
        w_hi = sb("w_hi", [P, KC, D], F32R)
        w_lo = sb("w_lo", [P, KC, D], F32R)
        w1_sb = sb("w1_sb", [P, KC, H])
        b1_sb = sb("b1_sb", [P, H])
        dinv = sb("dinv", [P, NT])
        run_end = sb("run_end", [P, 2, NT + 1], I32)
        fan = sb("fan", [P, NT + 1])
        edge = sb("edge", [P, 2, 3, ET])
        edge_row = sb("edge_row", [P, 2, ET], I32)
        x_t = sb("x_t", [P, 2, D])
        z_t = sb("z_t", [P, 2, D])
        zT_hi = sb("zT_hi", [P, 2, KC, P], F32R)
        zT_lo = sb("zT_lo", [P, 2, KC, P], F32R)
        xb_t = sb("xb_t", [P, 2, D])
        y_t = sb("y_t", [P, 2, D])
        yT = sb("yT", [P, 2, KC, P])
        r_t = sb("r_t", [P, 2, H])
        end_idx = sb("end_idx", [P, 8], I32)
        stats = sb("stats", [P, 8, 6])
        mv = sb("mv", [P, 8, 2])
        sd = sb("sd", [P, 8])
        rstd = sb("rstd", [P, 8])
        shift = sb("shift", [P, 8])

        psum = ctx.enter_context(nc.psum_tensor("psum", [P, 8, 512], F32))

        key_col_i = scratch(2 * ET).bitcast(I32)[0:EP, :].rearrange("p (g t) -> p g t", g=2)
        ew_col = scratch(ET)[0:EP, :]
        cols = scratch(2 * ET)[0:EP, :].rearrange("p (g t) -> p g t", g=2)
        twice = scratch(ET)[0:EP, :]
        keys_even, keys_odd, keys_own = (scratch(E // 2).bitcast(I16)[0:EP, :] for n in range(3))
        below16 = scratch(P // 2).bitcast(I16)
        shifted = scratch(ET)[0:EP, :]
        unused = scratch(E).bitcast(BF16).rearrange("p (s e) -> p s e", s=2)
        tally = scratch(3 * ET)[0:EP, :].rearrange("p (v t) -> p v t", v=3)
        iota16 = scratch(P // 2).bitcast(BF16)
        ints = scratch(4 * ET).bitcast(I32).rearrange("p (s g t) -> p s g t", s=2, g=2)
        parts = scratch(4 * ET).rearrange("p (s g t) -> p s g t", s=2, g=2)
        rank_ints = scratch(2 * ET).bitcast(I32).rearrange("p (s t) -> p s t", s=2)
        greater = scratch(ET)[0:EP, :]
        rank_parts = scratch(ET).bitcast(BF16).rearrange("p (s t) -> p s t", s=2)
        parts16 = scratch(2 * ET).bitcast(BF16).rearrange("p (v t) -> p v t", v=4)
        hot_lo = scratch(ET * P // 2).bitcast(BF16).rearrange("p (t c) -> p t c", t=ET)
        hot_hi = scratch(ET * ET // 2).bitcast(BF16).rearrange("p (t c) -> p t c", t=ET)
        placed = scratch(5 * ET * ET // 2).bitcast(BF16).rearrange("p (t v c) -> p t v c", t=ET, v=5)
        placed_weights = scratch(3 * ET * ET // 2).bitcast(BF16).rearrange("p (t v c) -> p t v c", t=ET, v=3)
        sorted_parts = scratch(4 * ET).rearrange("p (h g t) -> p h g t", h=2, g=2)
        gathered_words = scratch(ET * D)
        gathered = gathered_words.rearrange("p (t c) -> p t c", t=ET)
        node_lo = [gathered_words[:, ET * (D - P):].rearrange("p (t c) -> p t c", t=ET),
                   scratch(ET * P // 2).bitcast(BF16).rearrange("p (t c) -> p t c", t=ET)]
        node_values_words = scratch(2 * ET * NT)
        node_values = node_values_words.rearrange("p (t v c) -> p t v c", t=ET, v=2)
        unused_by_act = [a[0:EP, 0:E].bitcast(BF16).rearrange("p (s e) -> p s e", s=2)
                         for a in (gathered_words, node_values_words)]
        src_hi = scratch(ET * NT // 2).bitcast(BF16).rearrange("p (t c) -> p t c", t=ET)
        count_ = scratch(2 * NT).rearrange("p (g c) -> p g c", g=2)
        degree = scratch(2 * NT).rearrange("p (s c) -> p s c", s=2)
        half = scratch(NT)
        guess = scratch(NT)
        flat = scratch(4 * NT).rearrange("p (s g c) -> p s g c", s=2, g=2)
        row_lo = key_row_i[:, 0, :]
        src_hot = scratch(E // 2).bitcast(BF16)
        dinv_parts = scratch(3 * NT // 2 + 1).bitcast(BF16)[:, 0:3 * NT].rearrange("p (v c) -> p v c", v=3)
        rest = scratch(NT)
        look_words = scratch(ET * NT)
        look_prod = look_words.rearrange("p (t c) -> p t c", t=ET)
        unused_own = look_words[0:EP, 0:E // 2].bitcast(BF16)
        weight_parts = scratch(3 * ET // 2).bitcast(BF16).rearrange("p (v t) -> p v t", v=3)
        src_inv = scratch(ET)
        w_f = scratch(KC * D).rearrange("p (c n) -> p c n", c=KC)
        ends2 = run_end[:, 1, :]
        matches = xb_t[:].rearrange("p s (h m c) -> p (s h) m c", h=2, m=2)
        same = matches[:, :, 0, :]
        open_run = matches[:, :, 1, :]
        sum_t = y_t
        prev_key = sb("prev_key", [P, 2])
        M2 = 4
        NG = -(-NT // M2)
        LAST = NT - (NG - 1) * M2
        v_t = [buf[:, n, :] for buf in (x_t, xb_t, y_t, z_t) for n in range(2)]
        w2_parts = w_hi[0:S3, 0, :]
        w2_f = z_t[0:S3, 0, :]
        w2_h = w_lo[0:S3, 1, :]
        w2_l = z_t[0:S3, 1, :]
        is_mid = y_t[0:S3, 0, D - 2:D]
        spare = yT[:].rearrange("p s c n -> p (s c n)")
        hid_t = spare[:, 0:2 * M2 * H].rearrange("p (s j c) -> p s j c", s=2, j=M2)
        agg_t = spare[:, 2 * M2 * H:4 * M2 * H].rearrange("p (s j c) -> p s j c", s=2, j=M2)
        sum33 = spare[:, 4 * M2 * H:4 * M2 * H + 2 * M2 * K2].rearrange("p (s j c) -> p s j c", s=2, j=M2)
        split = w_lo[:, 2:4, 0:M2 * S3].rearrange("p s (j h c) -> p s j h c", j=M2, h=3)
        splitT = zT_hi[0:S3, :, :, :]

        BY_DVE = 1

        def summed_at(k, j):
            return psum[:, (2, 5)[k] + j - BY_DVE, :]

        def gathered1(t):
            per = D // H
            return x_t[:, t // per, t % per * H:(t % per + 1) * H]

        edges_in = sem("edges_in")
        rows_in = sems("rows_in", 2)
        weights_in = sem("weights_in")
        small_in = sem("small_in")
        w2_in = sem("w2_in")
        iotas_done = sem("iotas_done")
        dve_seq = sem("dve_seq")
        dve_consts = sem("dve_consts")
        col_parts = sem("col_parts")
        keys_ready = sem("keys_ready")
        tallied = sem("tallied")
        tallied_own = sem("tallied_own")
        tallied_by_act = sem("tallied_by_act")
        placed_ready = sem("placed_ready")
        permuted = sem("permuted")
        edges_sorted = sem("edges_sorted")
        hist_ready = sem("hist_ready")
        src_hist_ready = sem("src_hist_ready")
        hist_done = sem("hist_done")
        hist_taken = sem("hist_taken")
        counts_taken = sem("counts_taken")
        prefix_step = sem("prefix_step")
        prefix_ready = sem("prefix_ready")
        prefix_done = sem("prefix_done")
        ends_ready = sem("ends_ready")
        degree_ready = sem("degree_ready")
        degree_root = sem("degree_root")
        src_hot_ready = sem("src_hot_ready")
        dinv_ready = sem("dinv_ready")
        looked_up = sem("looked_up")
        weights_placed = sem("weights_placed")
        weights_permuted = sem("weights_permuted")
        edge_rows_in = [sems("edge_rows_in", ET), sems("edge_hid_in", ET)]
        key_row = sem("key_row")
        weights_taken = sem("weights_taken")
        w_split = sem("w_split")
        same_ready = sem("same_ready")
        tile_summed = sem("tile_summed")
        sum_copied = sem("sum_copied")
        sum_stored = sems("sum_stored", 2)
        x_in = sems("x_in", 2)
        end_prep = sem("end_prep")
        acc_in = sems("acc_in", 2)
        xb_done = sem("xb_done")
        z_done = sem("z_done")
        zT_done = sem("zT_done")
        hi_done = sem("hi_done")
        lo_done = sem("lo_done")
        prod_done = sem("prod_done")
        u_done = sem("u_done")
        stats_done = sem("stats_done")
        mv_done = sem("mv_done")
        sd_done = sem("sd_done")
        rstd_done = sem("rstd_done")
        shift_done = sem("shift_done")
        y_done = sem("y_done")
        y_kept = sems("y_kept", 2)
        yT_done = sem("yT_done")
        yT_copied = sem("yT_copied")
        pre_done = sem("pre_done")
        pre_taken = sem("pre_taken")
        r_done = sem("r_done")
        r_stored = sems("r_stored", 2)
        hid_in = sems("hid_in", 2)
        end_prep2 = sem("end_prep2")
        count_put = sem("count_put")
        agg_in = sems("agg_in", 2)
        add_done = sem("add_done")
        hi2_done = sem("hi2_done")
        split_done = sem("split_done")
        splitT_done = sem("splitT_done")
        splitT_copied = sem("splitT_copied")
        prod2_done = sem("prod2_done")
        with_y1 = sem("with_y1")
        v_done = sem("v_done")
        stats2_done = sem("stats2_done")
        mv2_done = sem("mv2_done")
        sd2_done = sem("sd2_done")
        rstd2_done = sem("rstd2_done")
        shift2_done = sem("shift2_done")
        out_done = sem("out_done")
        out_stored = sems("out_stored", 2 * M2)

        def key_row_at(t):
            return psum[:, t % 4, 0:P]

        block = ctx.enter_context(nc.Block())

        @block.sync
        def _(sp):
            for g, a in enumerate((dst, src)):
                sp.dma_start(key_col_i[:, g, :], a.rearrange("(p t) -> p t", p=EP)).then_inc(edges_in, 16)
            sp.dma_start(ew_col, ew.rearrange("(p t) -> p t", p=EP)).then_inc(edges_in, 16)
            for g, a in enumerate((dst, src)):
                sp.dma_start(key_row_i[:, g, :], a.rearrange("(a e) -> a e", a=1).to_broadcast([P, E])).then_inc(rows_in[g], 16)
            sp.dma_start(w_f, w.rearrange("(c p) n -> p c n", p=P)).then_inc(weights_in, 16)
            sp.dma_start(bias[:], b.rearrange("(a n) -> a n", a=1).to_broadcast([P, D])).then_inc(small_in, 16)
            sp.dma_start(w1_sb[:], w1.rearrange("(c p) n -> p c n", p=P)).then_inc(small_in, 16)
            sp.dma_start(b1_sb[:], b1.rearrange("(a n) -> a n", a=1).to_broadcast([P, H])).then_inc(small_in, 16)

            def load_x(q, k):
                t = 2 * q + k
                wait(sp, z_done, t - 1)
                wait(sp, xb_done, t - 1)
                if isinstance(t, int) and t == NT - 1:
                    sp.dma_start(x_t[0:TAIL, k, :], x[t * P:N, :]).then_inc(x_in[k], 16)
                else:
                    sp.dma_start(x_t[:, k, :], x[bass.ds(t * P, P), :]).then_inc(x_in[k], 16)

            load_x(0, 0)
            load_x(0, 1)

            def store_sum(g, t):
                sp.wait_ge(sum_copied, g * ET + t + 1)
                dest, cols_ = ((sums0, D), (sums1, H))[g]
                sp.dma_start(dest[t * P:(t + 1) * P, :], sum_t[:, t % 2, 0:cols_]).then_inc(sum_stored[t % 2], 16)

            for t in range(ET):
                store_sum(0, t)

            def layer1_step(q, k):
                s = 2 * q + k
                static = isinstance(s, int)
                if not static or s + 2 < NT:
                    load_x(*before(q, k, -2, 2))
                if not static or 0 <= s - 2 < NT:
                    t, kk = s - 2, k
                    sp.wait_ge(y_done, t + 1)
                    sp.dma_start(Y[:, bass.ds(t * D, D)], y_t[:, kk, :]).then_inc(y_kept[kk], 16)
                if not static or 0 <= s - 4 < NT:
                    t, kk = s - 4, k
                    sp.wait_ge(r_done, t + 1)
                    if static and t == NT - 1:
                        sp.dma_start(hidden[t * P:N, :], r_t[0:TAIL, kk, :]).then_inc(r_stored[kk], 16)
                    else:
                        sp.dma_start(hidden[bass.ds(t * P, P), :], r_t[:, kk, :]).then_inc(r_stored[kk], 16)

            steps(sp, NT + 4, 6, 8, 2, layer1_step)

            sp.wait_ge(prod_done, NT)
            for c in range(3):
                sp.dma_start(w2_f[c * K2:c * K2 + H, :], w2).then_inc(w2_in, 16)
                sp.dma_start(w2_f[c * K2 + H:(c + 1) * K2, :], b2.rearrange("(a n) -> a n", a=1)).then_inc(w2_in, 16)

            for t in range(ET):
                store_sum(1, t)

            def load_hidden(q, k):
                g = 2 * q + k
                wait(sp, add_done, g - 1)
                if isinstance(g, int) and g == NG - 1:
                    for j in range(LAST):
                        t = g * M2 + j
                        n = TAIL if t == NT - 1 else P
                        sp.dma_start(hid_t[0:n, k, j, :], hidden[t * P:t * P + n, :]).then_inc(hid_in[k], 16)
                else:
                    sp.dma_start(hid_t[:, k, :, :], hidden[bass.ds(g * (M2 * P), M2 * P), :].rearrange(
                        "(j p) h -> p j h", p=P)).then_inc(hid_in[k], 16)

            for k in range(2):
                sp.wait_ge(r_stored[k], 16 * ((NT - k + 1) // 2))
            load_hidden(0, 0)
            load_hidden(0, 1)
            load_hidden(1, 0)

            def store_group(q, k):
                g = 2 * q + k
                static = isinstance(g, int)
                if not static or g + 3 < NG:
                    load_hidden(*before(q, k, -3, 2))
                for j in range(LAST if static and g == NG - 1 else M2):
                    t = g * M2 + j
                    n = k * M2 + j
                    sp.wait_ge(out_done, t + 1)
                    if static and t == NT - 1:
                        sp.dma_start(out[t * P:N, :], v_t[n][0:TAIL, :]).then_inc(out_stored[n], 16)
                    else:
                        sp.dma_start(out[bass.ds(t * P, P), :], v_t[n]).then_inc(out_stored[n], 16)

            steps(sp, NG, 2, 5, 2, store_group)
            for n in range(2 * M2):
                sp.wait_ge(out_stored[n], 16 * len(range(n, NT, 2 * M2)))

        @block.gpsimd
        def _(pool):
            pool.iota(iota_col, [[1, P]], base=0, channel_multiplier=0,
                      allow_small_or_imprecise_dtypes=True).then_inc(iotas_done, 1)
            pool.iota(iota_part[:], [[0, 1]], base=0, channel_multiplier=1,
                      allow_small_or_imprecise_dtypes=True).then_inc(iotas_done, 1)

            pool.wait_ge(col_parts, 1)
            for t in range(ET):
                pool.tensor_scalar(node_values[0:EP, t, 0, :], iota_col[0:EP, 0:NT], parts[0:EP, 0, 0, t:t + 1], None,
                                   ALU.is_equal)
                pool.tensor_scalar(node_values[0:EP, t, 1, :], iota_col[0:EP, 0:NT], parts[0:EP, 0, 0, t:t + 1],
                                   ew_col[:, t:t + 1], ALU.is_equal, ALU.mult)
                pool.tensor_scalar(node_lo[0][0:EP, t, :], iota_col[0:EP, 0:P], parts[0:EP, 1, 0, t:t + 1], None,
                                   ALU.is_equal).then_inc(hist_ready, 1)

            pool.wait_ge(edges_sorted, 1)
            for t in range(ET):
                pool.indirect_dma_start(gathered[:, t, :], None, x,
                                        bass.IndirectOffsetOnAxis(ap=edge_row[:, 0, t:t + 1], axis=0),
                                        bounds_check=N - 1, oob_is_err=False).then_inc(edge_rows_in[0][t], 16)

            for t in range(ET):
                last = pool.tensor_scalar(node_lo[1][0:EP, t, :], iota_col[0:EP, 0:P], parts[0:EP, 1, 1, t:t + 1], None,
                                          ALU.is_equal)
            last.then_inc(src_hist_ready, 1)
            pool.wait_ge(counts_taken, 1)
            pool.memset(flat[:, 0, :, 0:1], 0.0)
            pool.tensor_copy(flat[:, 0, :, 1:NT], count_[:, :, 0:NT - 1]).then_inc(prefix_step, 1)
            at, width, n = 0, 1, 1
            while width < NT:
                pool.wait_ge(prefix_step, n)
                pool.tensor_copy(flat[:, 1 - at, :, 0:width], flat[:, at, :, 0:width])
                pool.tensor_tensor(flat[:, 1 - at, :, width:NT], flat[:, at, :, width:NT],
                                   flat[:, at, :, 0:NT - width], ALU.add).then_inc(prefix_step, 1)
                at, width, n = 1 - at, 2 * width, n + 1
            pool.wait_ge(prefix_step, n)
            assert at == 1
            pool.tensor_scalar(flat[:, 0], count_, 0.0, NO_ROW, ALU.is_equal, ALU.mult).then_inc(prefix_ready, 1)

            last_sum = pool.to_reg(ET * P - 1)

            def node_sums(q, k):
                t = 2 * q + k
                static = isinstance(t, int)
                if not static or t < NT:
                    wait(pool, zT_done, t - 1)
                    pool.tensor_copy(end_idx[:, k:k + 1], run_end[:, 0, bass.ds(t, 1)]).then_inc(end_prep, 1)
                    pool.memset(z_t[:, k, :], 0.0).then_inc(end_prep, 1)
                    pool.wait_ge(end_prep, 2 * t + 2)
                if not static or t >= 2:
                    pool.wait_ge(x_in[k], 16 * q)
                    wait(pool, u_done, t - 3)
                    pool.tensor_tensor(xb_t[:, k, :], x_t[:, k, :], bias[:], ALU.add).then_inc(xb_done, 1)
                if not static or t < NT:
                    pool.indirect_dma_start(z_t[:, k, :], None, sums0,
                                            bass.IndirectOffsetOnAxis(ap=end_idx[:, k:k + 1], axis=0),
                                            bounds_check=last_sum, oob_is_err=False).then_inc(acc_in[k], 16)

            for k in range(2):
                pool.wait_ge(sum_stored[k], 16 * (ET // 2))
            pool.wait_ge(ends_ready, 1)
            pool.wait_ge(small_in, 16 * 3)
            steps(pool, NT + 2, 4, 3, 2, node_sums)

            for k in range(2):
                pool.wait_ge(r_stored[k], 16 * ((NT - k + 1) // 2))
            for t in range(ET):
                pool.indirect_dma_start(gathered1(t), None, hidden,
                                        bass.IndirectOffsetOnAxis(ap=edge_row[:, 1, t:t + 1], axis=0),
                                        bounds_check=N - 1, oob_is_err=False).then_inc(edge_rows_in[1][t], 16)

            def node_sums2(q, k):
                g = 2 * q + k
                static = isinstance(g, int)
                wait(pool, add_done, g - 1)
                pool.tensor_copy(end_idx[:, k * M2:(k + 1) * M2], ends2[:, bass.ds(g * M2, M2)]).then_inc(end_prep2, 1)
                pool.memset(agg_t[:, k, :, :], 0.0).then_inc(end_prep2, 1)
                pool.wait_ge(end_prep2, 2 * g + 2)
                wait(pool, split_done, g - 1)
                pool.tensor_copy(sum33[:, k, :, H], fan[:, bass.ds(g * M2, M2)]).then_inc(count_put, 1)
                if static and g == 0:
                    for parity in range(2):
                        pool.wait_ge(sum_stored[parity], 16 * ET)
                for j in range(LAST if static and g == NG - 1 else M2):
                    n = k * M2 + j
                    pool.indirect_dma_start(agg_t[:, k, j, :], None, sums1,
                                            bass.IndirectOffsetOnAxis(ap=end_idx[:, n:n + 1], axis=0),
                                            bounds_check=last_sum, oob_is_err=False).then_inc(agg_in[k], 16)

            steps(pool, NG, 4, 2, 2, node_sums2)

        @block.scalar
        def _(act):
            def tally_by_act(g, n, part):
                t = ACT_FROM + n
                if n == 0 and part == 0:
                    act.wait_ge(keys_ready, g + 1)
                wait(act, tallied_by_act, 2 * (g * NA + n - 1) if n > 1 else 2 * g * NA)
                here = slice(0, t * EP) if part == 0 else slice((t + 1) * EP, E)
                nc.scalar.activation(unused_by_act[g][:, n % 2, here], (keys_even, keys_odd)[part][:, here], ACT.Sign,
                                     bias=shifted[:, t:t + 1], accum_out=tally[:, 2 * part, t:t + 1]).then_inc(tallied_by_act, 1)

            for n in range(NA):
                for part in range(2):
                    tally_by_act(0, n, part)
            act.wait_ge(degree_ready, 1)
            nc.scalar.activation(degree[:, 1, :], degree[:, 1, :], ACT.Sqrt).then_inc(degree_root, 1)

            def copy_sum(g, t):
                act.wait_ge(tile_summed, g * ET + t + 1)
                n = g * (ET // 2) + t // 2
                wait(act, sum_stored[t % 2], 16 * n)
                c = (D, H)[g]
                nc.scalar.copy(sum_t[:, t % 2, 0:c], psum[:, 6 + t % 2, 0:c]).then_inc(sum_copied, 1)

            for t in range(ET):
                copy_sum(0, t)
                if 0 <= t - 2 < 2 * NA:
                    tally_by_act(1, (t - 2) // 2, t % 2)

            def layer1_step(q, k):
                s = 2 * q + k
                static = isinstance(s, int)
                if not static or s < NT:
                    act.wait_ge(zT_done, s + 1)
                    wait(act, prod_done, s - 1)
                    nc.scalar.copy(zT_hi[:, k, :, :].rearrange("p c n -> p (c n)"), psum[:, k, :]).then_inc(hi_done, 1)
                if not static or 0 <= s - 3 < NT:
                    t, kk = s - 3, (k - 3) % 2
                    act.wait_ge(yT_done, t + 1)
                    wait(act, pre_done, t - 1)
                    nc.scalar.copy(yT[:, kk, :, :].rearrange("p c n -> p (c n)"), psum[:, 4 + kk, :]).then_inc(yT_copied, 1)
                if not static or 0 <= s - 4 < NT:
                    t, kk = s - 4, k
                    act.wait_ge(pre_taken, t + 1)
                    nc.scalar.activation(r_t[:, kk, :], r_t[:, kk, :], ACT.Relu).then_inc(r_done, 1)
                if not static or 0 <= s - 2 < NT:
                    t, kk = s - 2, k
                    act.wait_ge(mv_done, t + 1)
                    nc.scalar.activation(sd[:, kk:kk + 1], mv[:, kk, 1:2], ACT.Sqrt, bias=eps[:, 0:1]).then_inc(sd_done, 1)
                    act.wait_ge(shift_done, t + 1)
                    nc.scalar.activation(y_t[:, kk, :], y_t[:, kk, :], ACT.Identity, bias=shift[:, kk:kk + 1],
                                         scale=rstd[:, kk:kk + 1]).then_inc(y_done, 1)

            steps(act, NT + 4, 8, 5, 4, in_fours(layer1_step))

            for t in range(ET):
                copy_sum(1, t)

            def copy_splits(q, k):
                g = 2 * q + k
                act.wait_ge(splitT_done, g + 1)
                wait(act, with_y1, (g - 1) * (M2 - BY_DVE))
                nc.scalar.copy(splitT[:, k, :, :].rearrange("p c n -> p (c n)"), psum[0:S3, 1, :]).then_inc(splitT_copied, 1)

            def layer2_group(q, k):
                g = 2 * q + k
                static = isinstance(g, int)
                has_next = not static or g + 1 < NG
                if static and g == 0:
                    copy_splits(q, k)
                if not static or g - 1 >= 0:
                    kk = 1 - k
                    tiles = LAST if static and g == NG else M2
                    these = slice(kk * M2, (kk + 1) * M2)
                    act.wait_ge(mv2_done, (g - 1) * M2 + tiles)
                    nc.scalar.activation(sd[:, these], mv[:, these, 1], ACT.Sqrt, bias=eps[:, 0:1]).then_inc(sd2_done, 1)
                    act.wait_ge(shift2_done, g)
                    for j in range(tiles):
                        if j == 2 and has_next:
                            copy_splits(*before(q, k, -1, 2))
                        n = kk * M2 + j
                        if j >= BY_DVE:
                            wait(act, out_stored[n], 16 * (q if k == 1 else q - 1))
                        nc.scalar.activation(v_t[n], v_t[n] if j < BY_DVE else summed_at(kk, j), ACT.Identity,
                                             bias=shift[:, n:n + 1], scale=rstd[:, n:n + 1]).then_inc(out_done, 1)
                elif has_next:
                    copy_splits(*before(q, k, -1, 2))

            steps(act, NG + 1, 4, 3, 4, in_fours(layer2_group))

        @block.vector
        def _(dve):
            seq = [0]

            def then(ins):
                seq[0] += 1
                ins.then_inc(dve_seq, 1)
                dve.wait_ge(dve_seq, seq[0])

            dve.memset(ones, 1.0)
            dve.memset(eps[:], EPS)
            dve.memset(fan[:], 1.0)
            dve.memset(run_end[:, 1, NT:NT + 1], 0)
            dve.wait_ge(iotas_done, 2)
            dve.tensor_scalar(ident[:], iota_col, iota_part[:, 0:1], None, ALU.is_equal)
            dve.tensor_scalar(below, iota_col, iota_part[:, 0:1], None, ALU.is_gt)
            dve.tensor_scalar(below16, iota_col, iota_part[:, 0:1], None, ALU.is_gt)
            dve.memset(tally[:, 0, 0:1], 0.0)
            dve.memset(tally[:, 2, ET - 1:ET], 0.0)
            then(dve.tensor_scalar(last_row[:], iota_part[:], float(P - 1), None, ALU.is_equal))
            dve.memset(prev_key[:], 0.0).then_inc(dve_consts, 1)
            dve.wait_ge(edges_in, 48)
            dve.tensor_copy(cols, key_col_i)
            dve.tensor_scalar(ints[0:EP, 1], key_col_i, P - 1, None, ALU.bitwise_and)
            then(dve.tensor_scalar(ints[0:EP, 0], key_col_i, 7, None, ALU.logical_shift_right))
            dve.tensor_copy(parts[0:EP], ints[0:EP]).then_inc(col_parts, 1)
            dve.tensor_copy(parts16[0:EP], ints[0:EP].rearrange("p h g t -> p (h g) t"))
            dve.tensor_copy(iota16, iota_col)

            def widen_keys(g):
                dve.tensor_scalar(twice, cols[:, g, :], 2.0, None, ALU.mult)
                dve.tensor_scalar(shifted, cols[:, g, :], -2.0, -0.5, ALU.mult, ALU.add)
                dve.wait_ge(rows_in[g], 16)
                then(dve.tensor_scalar(keys_even.rearrange("q (t p) -> q t p", t=ET),
                                       key_row_i[0:EP, g, :].rearrange("q (p t) -> q t p", t=ET), 2.0, None, ALU.mult))
                then(dve.tensor_scalar(keys_odd, keys_even, 1.0, None, ALU.add))
                dve.tensor_tensor(keys_own.rearrange("q (t p) -> q t p", t=ET), keys_even.rearrange("q (t p) -> q t p", t=ET),
                                  below16[0:EP, None, 0:EP].to_broadcast([EP, ET, EP]), ALU.add).then_inc(keys_ready, 1)

            def tally_tile(g, n):
                t = DVE_TILES[n]
                wait(dve, tallied, g * ND + max(n - 1, 0))
                for part, keys, here in ((0, keys_even, slice(0, t * EP)), (2, keys_odd, slice((t + 1) * EP, E))):
                    if here.stop > here.start:
                        last = dve.tensor_scalar(unused[0:EP, n % 2, here], keys[:, here], twice[:, t:t + 1], None,
                                                 ALU.is_gt, ALU.add, accum_out=tally[:, part, t:t + 1])
                last.then_inc(tallied, 1)

            def tally_own(g, tiles):
                dve.wait_ge(keys_ready, g + 1)
                for t in tiles:
                    here = slice(t * EP, (t + 1) * EP)
                    dve.tensor_scalar(unused_own[:, here], keys_own[:, here], twice[:, t:t + 1], None,
                                      ALU.is_gt, ALU.add, accum_out=tally[:, 1, t:t + 1]).then_inc(tallied_own, 1)

            def place_edges(g):
                dve.wait_ge(tallied, (g + 1) * ND)
                dve.wait_ge(tallied_own, (g + 1) * ET)
                dve.wait_ge(tallied_by_act, (g + 1) * 2 * NA)
                by_act = slice(ACT_FROM, ACT_TO)
                then(dve.tensor_tensor(greater, tally[:, 0, :], tally[:, 2, :], ALU.add))
                then(dve.tensor_scalar(greater[:, by_act], greater[:, by_act], 0.5, 0.5 * (E - EP), ALU.mult, ALU.add))
                then(dve.tensor_tensor(greater, greater, tally[:, 1, :], ALU.add))
                then(dve.tensor_scalar(rank_ints[0:EP, 0, :], greater, -1.0, float(E - 1), ALU.mult, ALU.add))
                dve.tensor_scalar(rank_ints[0:EP, 1, :], rank_ints[0:EP, 0, :], P - 1, None, ALU.bitwise_and)
                then(dve.tensor_scalar(rank_ints[0:EP, 0, :], rank_ints[0:EP, 0, :], 7, None, ALU.logical_shift_right))
                then(dve.tensor_copy(rank_parts[0:EP], rank_ints[0:EP]))
                then(dve.tensor_tensor(hot_hi[0:EP], iota16[0:EP, None, 0:ET].to_broadcast([EP, ET, ET]),
                                       rank_parts[0:EP, 0, :, None].to_broadcast([EP, ET, ET]), ALU.is_equal))
                dve.tensor_tensor(placed[0:EP, :, 0:4, :], hot_hi[0:EP, :, None, :].to_broadcast([EP, ET, 4, ET]),
                                  parts16[0:EP].rearrange("p v t -> p t v")[:, :, :, None].to_broadcast([EP, ET, 4, ET]), ALU.mult)
                if g == 1:
                    dve.tensor_copy(placed[0:EP, :, 4, :], hot_hi[0:EP])
                dve.tensor_tensor(hot_lo[0:EP], iota16[0:EP, None, 0:P].to_broadcast([EP, ET, P]),
                                  rank_parts[0:EP, 1, :, None].to_broadcast([EP, ET, P]), ALU.is_equal).then_inc(placed_ready, 1)

            def take_sorted(g):
                dve.wait_ge(permuted, g + 1)
                if g == 1:
                    dve.tensor_copy(edge[:, 1, 2, :], psum[:, 6, 4 * ET:5 * ET])
                then(dve.tensor_copy(sorted_parts.rearrange("p h g t -> p (h g t)"), psum[:, 6, 0:4 * ET]))
                for v, side in enumerate((g, 1 - g)):
                    last = dve.scalar_tensor_tensor(edge[:, g, v, :], sorted_parts[:, 0, side, :], float(P),
                                                    sorted_parts[:, 1, side, :], ALU.mult, ALU.add)
                then(last)
                dve.tensor_copy(edge_row[:, g, :], edge[:, g, 1, :]).then_inc(edges_sorted, 1)

            def split_in_three(to, values, rest_):
                then(dve.tensor_copy(to[0], values))
                then(dve.tensor_tensor(rest_, values, to[0], ALU.subtract))
                then(dve.tensor_copy(to[1], rest_))
                return dve.tensor_tensor(to[2], rest_, to[1], ALU.subtract)

            def src_one_hots():
                dve.wait_ge(rows_in[1], 16)
                then(dve.tensor_scalar(row_lo.rearrange("q (t p) -> q t p", t=ET),
                                       key_row_i[:, 1, :].rearrange("q (p t) -> q t p", t=ET),
                                       P - 1, None, ALU.bitwise_and))
                dve.tensor_scalar(src_hot, row_lo, iota_part[:, 0:1], None, ALU.is_equal).then_inc(src_hot_ready, 1)

            def src_upper():
                dve.tensor_tensor(src_hi[0:EP], iota16[0:EP, None, 0:NT].to_broadcast([EP, ET, NT]),
                                  parts16[0:EP, 1, :, None].to_broadcast([EP, ET, NT]), ALU.is_equal)

            def take_degree():
                dve.wait_ge(hist_done, 1)
                dve.tensor_copy(count_[:, 0, :], psum[:, 7, 0:NT])
                then(dve.tensor_scalar(degree[:, 0, :], psum[:, 7, NT:2 * NT], 1.0, None, ALU.add))
                dve.tensor_scalar(degree[:, 1, :], degree[:, 0, :], SMALLEST_DEGREE, None, ALU.max).then_inc(degree_ready, 1)
                dve.tensor_scalar(half, degree[:, 0, :], SMALLEST_DEGREE, -0.5, ALU.max, ALU.mult).then_inc(hist_taken, 1)

            def take_dinv():
                dve.wait_ge(degree_root, 1)
                then(dve.reciprocal(guess, degree[:, 1, :]))
                then(dve.tensor_tensor(half, half, guess, ALU.mult))
                then(dve.tensor_tensor(half, half, guess, ALU.mult))
                then(dve.scalar_tensor_tensor(guess, half, 1.5, guess, ALU.add, ALU.mult))
                then(dve.scalar_tensor_tensor(dinv[:], degree[:, 0, :], 0.0, guess, ALU.is_gt, ALU.mult))
                split_in_three([dinv_parts[:, v, :] for v in range(3)], dinv[:], rest).then_inc(dinv_ready, 1)

            def take_counts():
                dve.wait_ge(hist_done, 2)
                dve.tensor_copy(count_[:, 1, :], psum[:, 5, 0:NT])
                dve.tensor_scalar(fan[:, 0:NT], psum[:, 5, 0:NT], 1.0, None, ALU.add).then_inc(counts_taken, 1)

            def take_ends():
                dve.wait_ge(prefix_done, 1)
                dve.wait_ge(prefix_ready, 1)
                dve.scalar_tensor_tensor(run_end[:, :, 0:NT], psum[:, 4, 0:2 * NT].rearrange("p (g c) -> p g c", g=2), -1.0,
                                         flat[:, 0], ALU.add, ALU.add).then_inc(ends_ready, 1)

            def weigh_edges():
                for n, t in enumerate(range(0, ET, LOOKS)):
                    tiles = min(LOOKS, ET - t)
                    dve.wait_ge(looked_up, n + 1)
                    last = dve.tensor_tensor(look_prod[0:EP, t:t + tiles, :],
                                             psum[0:EP, 1 + n, 0:tiles * NT].rearrange("p (t c) -> p t c", t=tiles),
                                             src_hi[0:EP, t:t + tiles, :], ALU.mult)
                then(last)
                then(dve.tensor_reduce(src_inv[0:EP, :], look_prod[0:EP], AXIS.X, ALU.add))
                then(dve.tensor_tensor(src_inv[0:EP, :], src_inv[0:EP, :], ew_col, ALU.mult))
                then(split_in_three([weight_parts[0:EP, v, :] for v in range(3)], src_inv[0:EP, :], rest[0:EP, 0:ET]))
                dve.tensor_tensor(placed_weights[0:EP], hot_hi[0:EP, :, None, :].to_broadcast([EP, ET, 3, ET]),
                                  weight_parts[0:EP].rearrange("p v t -> p t v")[:, :, :, None].to_broadcast([EP, ET, 3, ET]),
                                  ALU.mult).then_inc(weights_placed, 1)

            def match_keys(g, t):
                k, n = t % 2, g * ET + t
                dve.wait_ge(key_row, n + 1)
                wait(dve, tile_summed, n - 3)
                wait(dve, same_ready, n)
                row = key_row_at(t)
                dve.tensor_scalar(same[:, t % 4, :], row, edge[:, g, 0, t:t + 1], edge[:, g, 2, t:t + 1],
                                  ALU.is_equal, ALU.mult)
                if t > 0:
                    dve.tensor_scalar(open_run[:, t % 4, :], row, prev_key[:, 1 - k:2 - k], last_row[:, 0:1],
                                      ALU.is_equal, ALU.mult)
                dve.tensor_copy(prev_key[:, k:k + 1], row[:, P - 1:P]).then_inc(same_ready, 1)

            widen_keys(0)
            for n in range(ND):
                tally_tile(0, n)
            tally_own(0, range(ET))
            place_edges(0)
            src_one_hots()
            take_degree()
            take_sorted(0)
            take_dinv()
            src_upper()
            dve.wait_ge(weights_in, 16)
            then(dve.tensor_copy(w_hi[:], w_f))
            dve.tensor_tensor(w_lo[:], w_f, w_hi[:].bitcast(F32), ALU.subtract).then_inc(w_split, 1)
            weigh_edges()
            dve.wait_ge(weights_permuted, 1)
            dve.tensor_reduce(edge[:, 0, 2, :], psum[:, 7, 0:3 * ET].rearrange("p (v t) -> p t v", v=3), AXIS.X,
                              ALU.add).then_inc(weights_taken, 1)
            dve.wait_ge(weights_taken, 1)
            match_keys(0, 0)
            own = 0
            for t in range(ET):
                if t + 1 < ET:
                    match_keys(0, t + 1)
                if t == 0:
                    widen_keys(1)
                elif t >= 2:
                    tiles = range((t - 2) * ND // (ET - 2), (t - 1) * ND // (ET - 2))
                    for n in tiles:
                        tally_tile(1, n)
                    if not tiles:
                        tally_own(1, range(own, min(own + 3, ET)))
                        own += 3
                if t == 11:
                    take_counts()
            tally_own(1, range(own, ET))
            take_ends()
            place_edges(1)

            def make_z(q, k):
                dve.wait_ge(x_in[k], 16 * (q + 1))
                dve.wait_ge(acc_in[k], 16 * (q + 1))
                t = 2 * q + k
                dve.scalar_tensor_tensor(z_t[:, k, :], x_t[:, k, :], dinv[:, bass.ds(t, 1)], z_t[:, k, :],
                                         ALU.mult, ALU.add).then_inc(z_done, 1)

            make_z(0, 0)

            def layer1_step(q, k):
                s = 2 * q + k
                static = isinstance(s, int)
                has_u = not static or 0 <= s - 2 < NT
                t, kk = s - 2, k
                if static and s == 1:
                    take_sorted(1)
                if has_u:
                    dve.wait_ge(prod_done, t + 1)
                    dve.wait_ge(xb_done, t + 1)
                    wait(dve, yT_done, t - 1)
                    wait(dve, y_kept[kk], 16 * (q - 1))
                    dve.scalar_tensor_tensor(y_t[:, kk, :], psum[:, 2 + kk, :], dinv[:, bass.ds(t, 1)], xb_t[:, kk, :],
                                             ALU.mult, ALU.add).then_inc(u_done, 1)
                    dve.wait_ge(u_done, t + 1)
                    dve.bn_stats(stats[:, kk, :], y_t[:, kk, :]).then_inc(stats_done, 1)
                    dve.wait_ge(iotas_done, 2)
                    dve.wait_ge(stats_done, t + 1)
                    dve.bn_aggr(mv[:, kk, :], stats[:, kk, :]).then_inc(mv_done, 1)
                if not static or s < NT:
                    dve.wait_ge(hi_done, s + 1)
                    wait(dve, prod_done, s - 1)
                    dve.tensor_tensor(zT_lo[:, k, :, :].rearrange("p c n -> p (c n)"), psum[:, k, :],
                                      zT_hi[:, k, :, :].rearrange("p c n -> p (c n)").bitcast(F32),
                                      ALU.subtract).then_inc(lo_done, 1)
                if not static or 0 <= s - 4 < NT:
                    dve.wait_ge(pre_done, s - 3)
                    wait(dve, r_stored[k], 16 * (q - 2))
                    dve.tensor_tensor(r_t[:, k, :], psum[:, 6 + k, 0:H], b1_sb[:], ALU.add).then_inc(pre_taken, 1)
                if has_u:
                    dve.wait_ge(sd_done, t + 1)
                    wait(dve, y_done, t - 1)
                    dve.reciprocal(rstd[:, kk:kk + 1], sd[:, kk:kk + 1]).then_inc(rstd_done, 1)
                    dve.wait_ge(rstd_done, t + 1)
                    dve.scalar_tensor_tensor(shift[:, kk:kk + 1], mv[:, kk, 0:1], -1.0, rstd[:, kk:kk + 1],
                                             ALU.mult, ALU.mult).then_inc(shift_done, 1)
                if not static or s + 1 < NT:
                    make_z(*before(q, k, -1, 2))

            steps(dve, NT + 4, 8, 5, 4, in_fours(layer1_step))

            dve.wait_ge(prod_done, NT)
            for t in range(ET):
                match_keys(1, t)
            dve.wait_ge(w2_in, 16 * 6)
            then(dve.tensor_copy(w2_h, w2_f))
            dve.tensor_scalar(is_mid[:, 0:1], iota_part[0:S3, :], float(K2), None, ALU.is_ge)
            then(dve.tensor_scalar(is_mid[:, 1:2], iota_part[0:S3, :], float(2 * K2), None, ALU.is_lt))
            then(dve.tensor_tensor(is_mid[:, 0:1], is_mid[:, 0:1], is_mid[:, 1:2], ALU.mult))
            then(dve.tensor_scalar(is_mid[:, 1:2], is_mid[:, 0:1], -1.0, 1.0, ALU.mult, ALU.add))
            then(dve.tensor_tensor(w2_l, w2_f, w2_h.bitcast(F32), ALU.subtract))
            then(dve.tensor_scalar(w2_l, w2_l, is_mid[:, 0:1], None, ALU.mult))
            then(dve.scalar_tensor_tensor(w2_parts, w2_h.bitcast(F32), is_mid[:, 1:2], w2_l, ALU.mult, ALU.add))

            def add_sums(q, k):
                g = 2 * q + k
                static = isinstance(g, int)
                if static and g == NG - 1:
                    dve.wait_ge(hid_in[k], 16 * (q + LAST))
                    dve.wait_ge(agg_in[k], 16 * (q * M2 + LAST))
                else:
                    dve.wait_ge(hid_in[k], 16 * (q + 1))
                    dve.wait_ge(agg_in[k], 16 * M2 * (q + 1))
                wait(dve, split_done, g - 1)
                dve.tensor_tensor(sum33[:, k, :, 0:H], hid_t[:, k, :, :], agg_t[:, k, :, :], ALU.add).then_inc(add_done, 1)

            def split_hi(q, k):
                g = 2 * q + k
                dve.wait_ge(add_done, g + 1)
                dve.wait_ge(count_put, g + 1)
                wait(dve, splitT_done, g - 1)
                dve.tensor_copy(split[:, k, :, 0:2, :],
                                sum33[:, k, :, None, :].to_broadcast([P, M2, 2, K2])).then_inc(hi2_done, 1)

            def split_lo(q, k):
                g = 2 * q + k
                dve.wait_ge(hi2_done, g + 1)
                dve.tensor_tensor(split[:, k, :, 2, :], sum33[:, k, :, :], split[:, k, :, 0, :].bitcast(F32),
                                  ALU.subtract).then_inc(split_done, 1)

            for part in (add_sums, split_hi, split_lo):
                part(0, 0)

            def layer2_group(q, k):
                g = 2 * q + k
                static = isinstance(g, int)
                tiles = 0 if static and g >= NG else LAST if static and g == NG - 1 else M2

                def make_v(j):
                    if j < tiles:
                        t, n = g * M2 + j, k * M2 + j
                        dve.wait_ge(prod2_done, g * BY_DVE + j + 1)
                        wait(dve, out_stored[n], 16 * q)
                        dve.tensor_tensor(v_t[n], psum[:, j, :], Y[:, bass.ds(t * D, D)], ALU.add).then_inc(v_done, 1)

                def take_stats(j):
                    if j < tiles:
                        n = k * M2 + j
                        if j < BY_DVE:
                            dve.wait_ge(v_done, g * BY_DVE + j + 1)
                            dve.bn_stats(stats[:, n, :], v_t[n]).then_inc(stats2_done, 1)
                        else:
                            dve.wait_ge(with_y1, g * (M2 - BY_DVE) + j - BY_DVE + 1)
                            dve.bn_stats(stats[:, n, :], summed_at(k, j)).then_inc(stats2_done, 1)

                def take_mv(j):
                    if 0 <= j < tiles:
                        t, n = g * M2 + j, k * M2 + j
                        value = t + 1 if static else dve.to_reg(t + 1)
                        dve.wait_ge(iotas_done, 2)
                        dve.wait_ge(stats2_done, value)
                        dve.bn_aggr(mv[:, n, :], stats[:, n, :]).then_inc(mv2_done, 1)

                last = slice((1 - k) * M2, (2 - k) * M2)
                has_last = not static or 0 <= g - 1 < NG
                has_next = not static or g + 1 < NG
                if has_next:
                    add_sums(*before(q, k, -1, 2))
                    split_hi(*before(q, k, -1, 2))
                if has_last:
                    dve.wait_ge(sd2_done, g)
                    wait(dve, out_done, (g - 2) * M2)
                    dve.reciprocal(rstd[:, last], sd[:, last]).then_inc(rstd2_done, 1)
                if has_next:
                    split_lo(*before(q, k, -1, 2))
                if has_last:
                    dve.wait_ge(rstd2_done, g)
                    dve.scalar_tensor_tensor(shift[:, last], mv[:, last, 0], -1.0, rstd[:, last],
                                             ALU.mult, ALU.mult).then_inc(shift2_done, 1)
                make_v(0)
                take_stats(0)
                take_stats(1)
                take_mv(0)
                take_stats(2)
                take_mv(1)
                take_stats(3)
                take_mv(2)
                take_mv(3)

            steps(dve, NG + 1, 4, 3, 4, in_fours(layer2_group))

        @block.tensor
        def _(pe):
            pe.wait_ge(dve_consts, 1)

            def permute(g):
                pe.wait_ge(placed_ready, g + 1)
                for t in range(ET):
                    mm = pe.matmul(psum[:, 6, 0:(4 + g) * ET], hot_lo[0:EP, t, :],
                                   placed[0:EP, t, 0:4 + g, :].rearrange("p v c -> p (v c)"), start=t == 0, stop=t == ET - 1)
                mm.then_inc(permuted, 1)

            def row_of(out_ap, column):
                return pe.matmul(out_ap, column.to_broadcast([P, P]), ident[:], start=True, stop=True)

            def sum_tile(g, t):
                c = (D, H)[g]
                k, n = t % 2, g * ET + t
                pe.wait_ge(same_ready, n + 1)
                pe.wait_ge(edge_rows_in[g][t], 16)
                wait(pe, sum_copied, n - 1)
                rows = gathered[:, t, :] if g == 0 else gathered1(t)
                mm = pe.matmul(psum[:, 6 + k, 0:c], same[:, t % 4, :], rows, start=True, stop=t == 0)
                if t == 0:
                    mm.then_inc(tile_summed, 1)
                if t + 2 < ET:
                    row_of(key_row_at(t + 2), edge[:, g, 0, t + 2:t + 3]).then_inc(key_row, 1)
                if t > 0:
                    pe.wait_ge(sum_copied, n)
                    pe.matmul(psum[:, 6 + k, 0:c], open_run[:, t % 4, :], sum_t[:, 1 - k, 0:c], start=False,
                              stop=True).then_inc(tile_summed, 1)

            for t in range(ET):
                pe.wait_ge(hist_ready, t + 1)
                mm = pe.matmul(psum[:, 7, 0:2 * NT], node_lo[0][0:EP, t, :],
                               node_values[0:EP, t, :, :].rearrange("p v c -> p (v c)"), start=t == 0, stop=t == ET - 1)
            mm.then_inc(hist_done, 1)
            permute(0)
            pe.wait_ge(src_hot_ready, 1)
            pe.wait_ge(dinv_ready, 1)
            for t in range(ET):
                for v in range(3):
                    mm = pe.matmul(psum[0:EP, 1 + t // LOOKS, t % LOOKS * NT:(t % LOOKS + 1) * NT],
                                   src_hot[:, t * EP:(t + 1) * EP], dinv_parts[:, v, :], start=v == 0, stop=v == 2)
                if t % LOOKS == LOOKS - 1 or t == ET - 1:
                    mm.then_inc(looked_up, 1)
            pe.wait_ge(hist_taken, 1)
            pe.wait_ge(weights_placed, 1)
            for t in range(ET):
                mm = pe.matmul(psum[:, 7, 0:3 * ET], hot_lo[0:EP, t, :],
                               placed_weights[0:EP, t, :, :].rearrange("p v c -> p (v c)"), start=t == 0, stop=t == ET - 1)
            mm.then_inc(weights_permuted, 1)

            pe.wait_ge(weights_taken, 1)
            for t in range(2):
                row_of(key_row_at(t), edge[:, 0, 0, t:t + 1]).then_inc(key_row, 1)
            for t in range(ET):
                sum_tile(0, t)
                if t == 9:
                    pe.wait_ge(src_hist_ready, 1)
                    for h in range(ET):
                        mm = pe.matmul(psum[:, 5, 0:NT], node_lo[1][0:EP, h, :], src_hi[0:EP, h, :], start=h == 0, stop=h == ET - 1)
                    mm.then_inc(hist_done, 1)
                if t == 15:
                    pe.wait_ge(prefix_ready, 1)
                    ends = psum[:, 4, 0:2 * NT]
                    pe.matmul(ends, ones, flat[:, 1].rearrange("p g c -> p (g c)"), start=True, stop=False)
                    pe.matmul(ends, below, count_.rearrange("p g c -> p (g c)"), start=False, stop=False)
                    pe.matmul(ends, ident[:], count_.rearrange("p g c -> p (g c)"), start=False, stop=True).then_inc(prefix_done, 1)

            def layer1_step(q, k):
                s = 2 * q + k
                static = isinstance(s, int)
                if not static or s < NT:
                    pe.wait_ge(z_done, s + 1)
                    wait(pe, hi_done, s - 1)
                    wait(pe, lo_done, s - 1)
                    for c in range(KC):
                        mm = pe.transpose(psum[:, k, c * P:(c + 1) * P], z_t[:, k, c * P:(c + 1) * P], ident[:])
                    mm.then_inc(zT_done, 1)
                if static and s == 0:
                    permute(1)
                if not static or 0 <= s - 3 < NT:
                    t, kk = s - 3, (k - 3) % 2
                    pe.wait_ge(y_done, t + 1)
                    wait(pe, yT_copied, t - 1)
                    for c in range(KC):
                        mm = pe.transpose(psum[:, 4 + kk, c * P:(c + 1) * P], y_t[:, kk, c * P:(c + 1) * P], ident[:])
                    mm.then_inc(yT_done, 1)
                if not static or 0 <= s - 1 < NT:
                    t, kk = s - 1, (k - 1) % 2
                    pe.wait_ge(hi_done, t + 1)
                    pe.wait_ge(lo_done, t + 1)
                    wait(pe, u_done, t - 1)
                    n = 0
                    for c in range(KC):
                        for a, bb in ((zT_hi, w_hi), (zT_hi, w_lo), (zT_lo, w_hi)):
                            mm = pe.matmul(psum[:, 2 + kk, :], a[:, kk, c, :], bb[:, c, :], start=n == 0, stop=n == 3 * KC - 1)
                            n += 1
                    mm.then_inc(prod_done, 1)
                if static and s == 3:
                    pe.wait_ge(edges_sorted, 2)
                if not static or 0 <= s - 3 < NT:
                    t, kk = s - 3, (k - 3) % 2
                    pe.wait_ge(yT_copied, t + 1)
                    wait(pe, pre_taken, t - 1)
                    pre = psum[:, 6 + kk, 0:H]
                    for c in range(KC):
                        mm = pe.matmul(pre, yT[:, kk, c, :], w1_sb[:, c, :], start=c == 0, stop=c == KC - 1)
                    mm.then_inc(pre_done, 1)

            pe.wait_ge(w_split, 1)
            pe.wait_ge(small_in, 16 * 3)
            steps(pe, NT + 4, 8, 5, 4, in_fours(layer1_step))

            for t in range(2):
                row_of(key_row_at(t), edge[:, 1, 0, t:t + 1]).then_inc(key_row, 1)
            for t in range(ET):
                sum_tile(1, t)

            def transpose_splits(q, k):
                g = 2 * q + k
                pe.wait_ge(split_done, g + 1)
                wait(pe, splitT_copied, g - 1)
                for j in range(M2):
                    mm = pe.transpose(psum[0:S3, 1, j * P:(j + 1) * P],
                                      split[:, k, j, :, :].rearrange("p h c -> p (h c)").bitcast(F32), ident[:])
                mm.then_inc(splitT_done, 1)

            def layer2_group(q, k):
                g = 2 * q + k
                static = isinstance(g, int)
                if static and g == 0:
                    transpose_splits(q, k)
                pe.wait_ge(splitT_copied, g + 1)
                for j in range(LAST if static and g == NG - 1 else M2):
                    if j < BY_DVE:
                        wait(pe, v_done, (g - 1) * BY_DVE + j + 1)
                        pe.matmul(psum[:, j, :], splitT[:, k, j, :], w2_parts, start=True, stop=True).then_inc(prod2_done, 1)
                    else:
                        wait(pe, out_done, (g - 2) * M2 + j + 1)
                        pe.matmul(summed_at(k, j), splitT[:, k, j, :], w2_parts, start=True, stop=False)
                        pe.matmul(summed_at(k, j), ident[:], Y[:, bass.ds((g * M2 + j) * D, D)], start=False,
                                  stop=True).then_inc(with_y1, 1)
                if not static or g + 1 < NG:
                    transpose_splits(*before(q, k, -1, 2))

            steps(pe, NG, 4, 2, 4, in_fours(layer2_group))


_INS = ['x', 'src', 'dst', 'edge_weight', 'L0_gnn_W', 'L0_gnn_b', 'L1_gnn_W1', 'L1_gnn_b1', 'L1_gnn_W2', 'L1_gnn_b2']


def kernel(**inputs):
    import numpy as _np
    import concourse.bacc as _bacc
    from concourse import mybir as _mybir
    from concourse.bass_utils import run_bass_kernel_spmd as _run

    nc = _bacc.Bacc("TRN2", target_bir_lowering=False, num_devices=1)
    arrays, args = {}, []
    for name in _INS:
        a = _np.ascontiguousarray(inputs[name])
        arrays[f"in_{name}_dram"] = a
        args.append(nc.dram_tensor(f"in_{name}_dram", a.shape, _mybir.dt.from_np(a.dtype), kind="ExternalInput").ap())
    out = nc.dram_tensor("out_0_dram", inputs["x"].shape, _mybir.dt.float32, kind="ExternalOutput").ap()
    graph_layers(nc, *args, out)
    r = _run(nc, [arrays], core_ids=[0])
    return r.results[0]["out_0_dram"]
```
